# Optimizing a Trainium2 kernel written in Bass

```python
import numpy as np
import jax
import jax.numpy as jnp

def _softmax(x, axis=-1):
    return jax.nn.softmax(x, axis=axis)

def _gelu(x):
    return jax.nn.gelu(x, approximate=True)

def _silu(x):
    return jax.nn.silu(x)

def _sigmoid(x):
    return jax.nn.sigmoid(x)

def _layernorm(x, axis=-1, eps=1e-05):
    m = jnp.mean(x, axis=axis, keepdims=True)
    v = jnp.var(x, axis=axis, keepdims=True)
    return (x - m) / jnp.sqrt(v + eps)

def _scatter_add(tgt, idx, src, axis=0):
    return tgt.at[idx].add(src)

def _segment_sum(src, seg, n):
    return jax.ops.segment_sum(src, seg, n)
kernel_name = 'mk_lm_tower_d1_tok_ids768_r4_114790'

def setup_inputs(seed: int=0):
    np.random.seed(seed)
    _w = jnp.asarray

    def _rec_inputs():
        import jax
        import jax.numpy as jnp
        _rk = jax.random.key(seed)
        x = jax.random.randint(jax.random.fold_in(_rk, 1), (4, 512), 0, 1114110, jnp.int32)
        return x
    x = _rec_inputs()

    def _L0_tok_setup():
        import jax, jax.numpy as jnp
        import numpy as np
        _PRIMES = [31, 43, 59, 61, 73, 97, 103, 113]
        NUM_HASHES = 8
        NUM_BUCKETS = 4096
        HIDDEN = 192
        SHARD = HIDDEN // NUM_HASHES
        BATCH, SEQ = (8, 2048)
        LN_EPS = 1e-06
        key = jax.random.key(seed)
        k_ids, k_tab, k_g, k_b = jax.random.split(key, 4)
        input_ids = jax.random.randint(k_ids, (BATCH, SEQ), 0, 278528, dtype=jnp.int64)
        tables = jax.random.normal(k_tab, (NUM_HASHES, NUM_BUCKETS, SHARD), dtype=jnp.float32)
        ln_scale = jnp.ones((HIDDEN,), dtype=jnp.float32)
        ln_bias = jnp.zeros((HIDDEN,), dtype=jnp.float32)
        return {'input_ids': input_ids, 'tables': tables, 'ln_scale': ln_scale, 'ln_bias': ln_bias}
    _L0_tok_all = _L0_tok_setup()
    _L0_tok_in = {k: v for k, v in _L0_tok_all.items() if k in ('tables', 'ln_scale', 'ln_bias')}
    del _L0_tok_all

    def _L0_attn_setup():
        import jax, jax.numpy as jnp
        import numpy as np
        NUM_HEADS = 12
        SCRA_SCALING = 10.0
        EPS = 1e-12
        key = jax.random.key(seed)
        ks = jax.random.split(key, 5)
        B, N, C = (2, 512, 192)
        return {'x': jax.random.normal(ks[0], (B, N, C), dtype=jnp.float32), 'qkv_w': jax.random.normal(ks[1], (3 * C, C), dtype=jnp.float32) * 0.02, 'qkv_b': jax.random.normal(ks[2], (3 * C,), dtype=jnp.float32) * 0.02, 'proj_w': jax.random.normal(ks[3], (C, C), dtype=jnp.float32) * 0.02, 'proj_b': jax.random.normal(ks[4], (C,), dtype=jnp.float32) * 0.02}
    _L0_attn_all = _L0_attn_setup()
    _L0_attn_in = {k: v for k, v in _L0_attn_all.items() if k in ('qkv_w', 'qkv_b', 'proj_w', 'proj_b')}
    del _L0_attn_all

    def _L0_ffn_setup():
        import jax, jax.numpy as jnp
        import numpy as np
        TOP_K = 2
        key = jax.random.key(seed)
        ks = jax.random.split(key, 5)
        B, S, D, H, E = (1, 512, 192, 768, 8)
        x = jax.random.normal(ks[0], (B, S, D), dtype=jnp.float32)
        gate_w = jax.random.normal(ks[1], (E, D), dtype=jnp.float32) * 0.02
        w1 = jax.random.normal(ks[2], (E, D, H), dtype=jnp.float32) * 0.02
        b1 = jnp.zeros((E, H), dtype=jnp.float32)
        w2 = jax.random.normal(ks[3], (E, H, D), dtype=jnp.float32) * 0.02
        b2 = jnp.zeros((E, D), dtype=jnp.float32)
        return {'x': x, 'gate_w': gate_w, 'w1': w1, 'b1': b1, 'w2': w2, 'b2': b2}
    _L0_ffn_all = _L0_ffn_setup()
    _L0_ffn_in = {k: v for k, v in _L0_ffn_all.items() if k in ('gate_w', 'w1', 'b1', 'w2', 'b2')}
    del _L0_ffn_all
    return {'x': x, 'L0_tok_tables': _L0_tok_in['tables'], 'L0_tok_ln_scale': _L0_tok_in['ln_scale'], 'L0_tok_ln_bias': _L0_tok_in['ln_bias'], 'L0_attn_qkv_w': _L0_attn_in['qkv_w'], 'L0_attn_qkv_b': _L0_attn_in['qkv_b'], 'L0_attn_proj_w': _L0_attn_in['proj_w'], 'L0_attn_proj_b': _L0_attn_in['proj_b'], 'L0_ffn_gate_w': _L0_ffn_in['gate_w'], 'L0_ffn_w1': _L0_ffn_in['w1'], 'L0_ffn_b1': _L0_ffn_in['b1'], 'L0_ffn_w2': _L0_ffn_in['w2'], 'L0_ffn_b2': _L0_ffn_in['b2']}

def reference(x, L0_tok_tables, L0_tok_ln_scale, L0_tok_ln_bias, L0_attn_qkv_w, L0_attn_qkv_b, L0_attn_proj_w, L0_attn_proj_b, L0_ffn_gate_w, L0_ffn_w1, L0_ffn_b1, L0_ffn_w2, L0_ffn_b2):
    import jax
    import jax.numpy as jnp

    def _L0_tok_ref(input_ids, tables, ln_scale, ln_bias):
        import jax, jax.numpy as jnp
        import numpy as np
        _PRIMES = [31, 43, 59, 61, 73, 97, 103, 113]
        NUM_HASHES = 8
        NUM_BUCKETS = 4096
        HIDDEN = 192
        SHARD = HIDDEN // NUM_HASHES
        BATCH, SEQ = (8, 2048)
        LN_EPS = 1e-06
        primes = jnp.asarray(_PRIMES, dtype=input_ids.dtype)
        hashed = (input_ids + 1)[None] * primes[:, None, None] % NUM_BUCKETS
        shards = jax.vmap(lambda tab, idx: tab[idx])(tables, hashed)
        emb = jnp.moveaxis(shards, 0, -2).reshape(input_ids.shape[0], input_ids.shape[1], HIDDEN)
        mean = jnp.mean(emb, axis=-1, keepdims=True)
        var = jnp.mean(jnp.square(emb - mean), axis=-1, keepdims=True)
        normed = (emb - mean) * jax.lax.rsqrt(var + LN_EPS)
        return normed * ln_scale + ln_bias

    def _L0_attn_ref(x, qkv_w, qkv_b, proj_w, proj_b):
        import jax, jax.numpy as jnp
        import numpy as np
        NUM_HEADS = 12
        SCRA_SCALING = 10.0
        EPS = 1e-12
        B, N, C = x.shape
        H = NUM_HEADS
        D = C // H
        scale = D ** (-0.5)
        xt = jnp.transpose(x, (1, 0, 2))
        qkv = xt @ qkv_w.T + qkv_b
        q, k, v = jnp.split(qkv, 3, axis=-1)

        def to_bh(t):
            return jnp.transpose(t.reshape(N, B * H, D), (1, 0, 2))
        q, k, v = (to_bh(q), to_bh(k), to_bh(v))
        attn = jax.nn.softmax(jnp.einsum('bnd,bmd->bnm', q, k) * scale, axis=-1)
        out = jnp.einsum('bnm,bmd->bnd', attn, v)
        out = jnp.transpose(out, (1, 0, 2)).reshape(N, B, C)
        out = out @ proj_w.T + proj_b
        out = jnp.transpose(out.reshape(N, B * H, D), (1, 0, 2))
        norm = jnp.linalg.norm(out, axis=-1, keepdims=True)
        sim_tokens = out / jnp.maximum(norm, EPS)
        sim = jnp.einsum('bnd,bmd->bnm', sim_tokens, sim_tokens) * SCRA_SCALING
        sim = jnp.where(sim < 0, -jnp.inf, sim)
        sim = jax.nn.softmax(sim, axis=-1)
        out2 = jnp.einsum('bnm,bmd->bnd', sim, v)
        out2 = jnp.transpose(out2, (1, 0, 2)).reshape(N, B, C)
        out2 = out2 @ proj_w.T + proj_b
        return jnp.transpose(out2, (1, 0, 2))

    def _L0_ffn_ref(x, gate_w, w1, b1, w2, b2):
        import jax, jax.numpy as jnp
        import numpy as np
        TOP_K = 2
        B, S, D = x.shape
        E, _, H = w1.shape
        T = B * S
        K = TOP_K
        xf = x.reshape(T, D)
        logits = xf @ gate_w.T
        probs = jax.nn.softmax(logits, axis=-1)
        top_w, top_i = jax.lax.top_k(probs, K)
        top_w = top_w / (jnp.sum(top_w, axis=-1, keepdims=True) + 1e-09)
        flat_e = top_i.reshape(-1)
        flat_w = top_w.reshape(-1)
        tok_idx = jnp.repeat(jnp.arange(T), K)
        order = jnp.argsort(flat_e)
        se = flat_e[order]
        pt = tok_idx[order]
        pw = flat_w[order]
        counts = jax.ops.segment_sum(jnp.ones(T * K, jnp.int32), se, num_segments=E)
        starts = jnp.concatenate([jnp.zeros((1,), jnp.int32), jnp.cumsum(counts)[:-1]])
        pos = jnp.arange(T * K) - starts[se]
        cap = T * K
        padded = jnp.zeros((E, cap, D), x.dtype).at[se, pos].set(xf[pt])
        hidden = jax.nn.gelu(jnp.einsum('ecd,edh->ech', padded, w1) + b1[:, None, :], approximate=False)
        out = jnp.einsum('ech,ehd->ecd', hidden, w2) + b2[:, None, :]
        expert_out = out[se, pos] * pw[:, None]
        final = jnp.zeros((T, D), x.dtype).at[pt].add(expert_out)
        return final.reshape(B, S, D)
    h = _L0_tok_ref(x, L0_tok_tables, L0_tok_ln_scale, L0_tok_ln_bias)
    h = h + _L0_attn_ref(_layernorm(h, axis=-1), L0_attn_qkv_w, L0_attn_qkv_b, L0_attn_proj_w, L0_attn_proj_b)
    h = h + _L0_ffn_ref(_layernorm(h, axis=-1), L0_ffn_gate_w, L0_ffn_w1, L0_ffn_b1, L0_ffn_w2, L0_ffn_b2)
    return h

_drawn_inputs = setup_inputs


def setup_inputs(seed=0):
    import zlib

    import numpy as np

    out = dict(_drawn_inputs(seed))
    spreads = {'L0_tok_ln_scale': (1.0, 0.2),
     'L0_tok_ln_bias': (0.0, 0.1),
     'L0_ffn_b1': (0.0, 0.393),
     'L0_ffn_b2': (0.0, 0.1)}
    factors = {'L0_attn_qkv_w': 5.092,
     'L0_attn_qkv_b': 8.0,
     'L0_attn_proj_w': 4.351,
     'L0_attn_proj_b': 2.673}
    for name, (base, spread) in spreads.items():
        noise = np.random.default_rng([zlib.crc32(name.encode()), seed]).standard_normal(out[name].shape)
        drawn = base * np.exp(spread * noise) if base else spread * noise
        out[name] = jnp.asarray(drawn.astype(out[name].dtype))
    for name, factor in factors.items():
        out[name] = (out[name] * factor).astype(out[name].dtype)
    return out
```

```python
from contextlib import ExitStack

import concourse.bass as bass
from concourse import mybir

F32 = mybir.dt.float32
F32R = mybir.dt.float32r
I32 = mybir.dt.int32
U32 = mybir.dt.uint32
ALU = mybir.AluOpType
ACT = mybir.ActivationFunctionType
AX_X = mybir.AxisListType.X

P = 128
B, N, C = 4, 512, 192
NH, D = 12, 16
BUCKETS = 4096
CT = N // P
TILES = B * CT
KC, KW = 2, 96
GH = 4
GB = NH // GH
NG = B * GB
UG = 2 * GH
VW = D + 1
E, HID = 8, 768
HC = HID // P
TOPK = 2
NBLK = (B * N * TOPK) // P + E - 1
DUMP = B * N
QSCALE = D ** -0.5
SIM_SCALE = 10.0
RING = 3
PRING = 6
RSQRT_MAGIC = 0x5F3759DF

OFF_C, OFF_E = 11, 46


def schedule():
    ev = []

    def at(t, rank, kind, *args):
        ev.append((t, rank, kind, args))

    for b in range(B):
        a = GB * UG * b
        first = b == 0
        at(-9 if first else a - 20, 0, "embed_norm", b)
        at(-8 if first else a - 17, 0, "attn_norm", b)
        at(-7 if first else a - 15, 0, "x_transpose", b)
        at(-6 if first else a - 14, 0, "q_proj", b)
        at(-5 if first else a - 13, 0, "k_proj", b)
        at(-4 if first else a - 12, 0, "v_proj", b)
        d = a + GB * UG - UG + OFF_C + UG + 3
        at(d + 1, 6, "o_transpose", b, 0)
        at(d + 2, 6, "proj_norm", b)
        at(d + 5, 6, "t_transpose", b)
        f = a + GB * UG - UG + OFF_E + UG + 4
        at(f + 1, 6, "o_transpose", b, 1)
        at(f + 2, 6, "proj_out", b)
        at(f + 5, 6, "gate_transpose", b)
        at(f + 6, 6, "gate_logits", b)
    for g in range(NG):
        a = UG * g
        at(-3 + g % GB if g < GB else a - 5, 1, "load_qk", g)
        for q in range(UG):
            at(a + q, 2, "max_unit", g, q)
            at(a + OFF_C + q, 3, "exp_unit", g, q)
            at(a + OFF_E + q, 4, "sim_unit", g, q)
            at(a + OFF_E + q + 1, 0, "mask", g, q)
        at(a + UG, 5, "max_row", g)
        for u in range(2):
            at(a + OFF_C + 5 + 4 * u, 5, "pv", g, u, 0)
            at(a + OFF_E + 6 + 4 * u, 5, "pv", g, u, 1)
        at(a + OFF_C + UG + 2, 5, "normalise", g, 0)
        at(a + OFF_E + UG + 3, 5, "normalise", g, 1)
        b = g // GB
        ready = GB * UG * b + GB * UG - UG + OFF_C + UG + 3 + 5
        at(max(ready, a + OFF_E - 9), 7, "load_sim", g)
    ev.sort(key=lambda e: (e[0], e[1]))
    return [(kind, args) for _, _, kind, args in ev]


EVENTS = schedule()
PSUM_KINDS = ("x_transpose", "q_proj", "k_proj", "v_proj", "max_unit", "max_row", "exp_unit", "normalise",
              "o_transpose", "proj_norm", "t_transpose", "sim_unit", "proj_out", "gate_transpose", "gate_logits")
UNIT = {ev: k for k, ev in enumerate(e for e in EVENTS if e[0] in PSUM_KINDS)}


def unit(kind, *args):
    return UNIT[(kind, args)]


def build(nc, ids, table, ln_scale, ln_bias, qkv_wt, qkv_b, proj_wt, proj_b, proj_wt_n, proj_b_n, gate_wt, w1, b1, w2, b2, out):
    ctx = ExitStack()
    with ctx:
        def sb(name, shape, dt=F32):
            return ctx.enter_context(nc.sbuf_tensor(name, shape, dt))

        def sem(name):
            return ctx.enter_context(nc.semaphore(name))

        x2_rows = nc.dram_tensor("x2_rows", (B * N, C), F32).ap()

        ident = sb("ident", [P, P])
        ids_sb = sb("ids_sb", [P, TILES], I32)
        rows_sb = sb("rows_sb", [P, TILES], I32)
        H = sb("H", [P, TILES, C])
        X = sb("X", [P, CT, C])
        X2 = sb("X2", [P, CT, C])
        scale_b = sb("scale_b", [P, C])
        bias_b = sb("bias_b", [P, C])
        stats = sb("stats", [P, CT, 6])
        mv = sb("mv", [P, CT, 2])
        nt = [sb(f"newton{i}", [P, CT * NH]) for i in range(4)]
        LG = sb("LG", [P, TILES, E])

        W1B = E * KC * HID
        arena1 = sb("arena1", [P, W1B])
        w1_sb = arena1[:, :].rearrange("p (e k h) -> p e k h", e=E, k=KC)
        at1 = [0]

        def carve(arena, pos, free):
            v = arena[:, pos[0]:pos[0] + free]
            pos[0] += free
            return v

        P1 = carve(arena1, at1, PRING * 2 * N).rearrange("p (s j n) -> p s j n", s=PRING, j=2)
        XT = carve(arena1, at1, KC * N).rearrange("p (k n) -> p k n", k=KC)
        WQKV = carve(arena1, at1, KC * 3 * C).rearrange("p (k m) -> p k m", k=KC)
        assert at1[0] <= W1B
        arena3 = sb("arena3", [P, 6 * KC * N])
        QK = {nm: arena3[0:KW, i * KC * N:(i + 1) * KC * N].rearrange("p (k n) -> p k n", k=KC)
              for i, nm in enumerate(("QH", "QL", "KH", "KL", "TH", "TL"))}
        QS = sb("QS", [112, GB, GH, N], F32R)
        KS = sb("KS", [112, GB, GH, N], F32R)
        w2_free = E * HC * C
        arena2 = sb("arena2", [P, B * CT * NH * VW + PRING * 2 * N + 2 * N])
        w2_sb = arena2[:, 0:w2_free].rearrange("p (e k d) -> p e k d", e=E, k=HC)
        at2 = [0]
        V = [carve(arena2, at2, CT * NH * VW).rearrange("p (c h w) -> p c h w", c=CT, h=NH) for _ in range(B)]
        P2 = carve(arena2, at2, PRING * 2 * N).rearrange("p (s j n) -> p s j n", s=PRING, j=2)
        ACCS = carve(arena2, at2, 2 * N).rearrange("p (s n) -> p s n", s=2)
        O = [sb(f"O{ps}", [P, CT, C]) for ps in range(2)]
        OT = sb("OT", [KW + 1, KC, N])
        T = sb("T", [P, CT, C])
        PW = sb("PW", [KW + 1, KC, C])
        PWN = sb("PWN", [KW + 1, KC, C])
        GT = sb("GT", [KW, KC, E])
        MX = sb("MX", [P, 2, 4 * GH])
        MRH = sb("MRH", [4 * GH, 2, P], F32R)
        MRL = sb("MRL", [4 * GH, 2, P], F32R)
        rec = sb("rec", [P, CT, GH])

        x_flat, x_at = X[:, :, :].rearrange("p c d -> p (c d)"), [0]

        zeros = sb("zeros", [P, C])
        ones = sb("ones", [P, P])
        before = sb("before", [P, P])
        slot_no = sb("slot_no", [P, P])
        block_no = sb("block_no", [P, NBLK])
        expert_no = sb("expert_no", [P, TILES, E])
        not_first = sb("not_first", [P, E, TILES])
        token_1 = sb("token_1", [P, TILES])
        dump_1 = sb("dump_1", [P, 1])
        rt = {nm: sb(f"rt_{nm}", [P, TILES, E]) for nm in ("a", "b", "oh0", "oh1", "prob")}
        col = {nm: sb(f"col_{nm}", [P, TILES]) for nm in ("m", "p0", "p1", "r")}
        weight = sb("weight", [P, TOPK, TILES])
        place = carve(x_flat, x_at, TOPK * TILES).rearrange("p (k t) -> p k t", k=TOPK)
        place_i = sb("place_i", [P, TOPK, TILES], I32)
        part_i = sb("part_i", [P, TOPK, TILES], I32)
        row_f = carve(x_flat, x_at, TOPK * TILES).rearrange("p (k t) -> p k t", k=TOPK)
        blk_f = carve(x_flat, x_at, TOPK * TILES).rearrange("p (k t) -> p k t", k=TOPK)
        exp8 = {nm: sb(f"exp8_{nm}", [P, E]) for nm in ("n", "end", "base")}
        exp8_i = sb("exp8_i", [P, E], I32)
        NQ = TOPK * TILES
        oh_blk = arena3[:, 0:NQ * NBLK].rearrange("p (q j) -> p q j", j=NBLK)
        tag = arena3[:, NQ * NBLK:3 * NQ * NBLK].rearrange("p (q s j) -> p q s j", s=2, j=NBLK)
        OHR = 8
        oh_row = arena3[:, 3 * NQ * NBLK:3 * NQ * NBLK + OHR * P].rearrange("p (s r) -> p s r", s=OHR)
        assert 3 * NQ * NBLK + OHR * P <= 6 * KC * N
        slot_token = sb("slot_token", [P, NBLK], I32)
        slot_dest = sb("slot_dest", [P, NBLK], I32)
        slot_weight = carve(x_flat, x_at, NBLK)
        slot_tmp = carve(x_flat, x_at, NBLK)
        blk_ge = carve(x_flat, x_at, NBLK * E)[0:1, :].rearrange("p (j e) -> p j e", e=E)
        blk_expert_f = carve(x_flat, x_at, NBLK)[0:1, :]
        blk_expert = sb("blk_expert", [1, NBLK], I32)
        at3 = [0]
        W1S = [carve(arena3, at3, KC * HID).rearrange("p (k h) -> p k h", k=KC) for _ in range(2)]
        HT = [carve(arena3, at3, HID).rearrange("p (k t) -> p k t", k=HC) for _ in range(2)]
        b2_b = carve(arena3, at3, E * C).rearrange("p (e d) -> p e d", e=E)
        XG = [T[:, i, :] for i in range(2)]
        XGT = [OT[:, :, i * P:(i + 1) * P] for i in range(2)]
        Y = [T[:, 2 + i, :] for i in range(2)]

        psum = ctx.enter_context(nc.psum_tensor("psum", [P, 8, N], F32))
        acc = [psum[:, 6, :], psum[:, 7, :]]

        def slot(k):
            return psum[:, 2 * (k % RING):2 * (k % RING) + 2, :]

        def slot4(k):
            return slot(k).rearrange("p j (c n) -> p (j c) n", c=2)

        def slot2(k, c):
            return slot(k)[:, c // 2, (c % 2) * C:(c % 2 + 1) * C]

        hid_ps = [psum[:, 2 * i:2 * i + 2, :].rearrange("p b n -> p (b n)")[:, 0:HID] for i in range(2)]
        xgt_ps = [psum[0:KW, 4 + i, 0:KC * P].rearrange("p (k t) -> p k t", k=KC) for i in range(2)]
        y_ps = [psum[:, 6 + i, 0:C] for i in range(2)]

        ids_in, lnw_in, wqkv_in, pw_in, gt_in = (sem(s) for s in ("ids_in", "lnw_in", "wqkv_in", "pw_in", "gt_in"))
        ident_set, consts_set, rows_ready = sem("ident_set"), sem("consts_set"), sem("rows_ready")
        gathered = [sem(f"gathered{b}") for b in range(B)]
        filled = [sem(f"psum_filled{s}") for s in range(RING)]
        freed = [sem(f"psum_freed{s}") for s in range(RING)]
        hi_written = sem("hi_written")
        normed_once, affine_done, x_ready = sem("normed_once"), sem("affine_done"), sem("x_ready")
        pool_step = sem("pool_step")
        max_done = sem("max_done")
        qk_loaded = [sem(f"qk_loaded{s}") for s in range(GB)]
        row_loaded = [sem(f"row_loaded{s}") for s in range(GB)]
        sim_loaded = [sem(f"sim_loaded{s}") for s in range(GB)]
        pv_done = [sem("pv1_done"), sem("pv2_done")]
        acc_saved = [sem("acc1_saved"), sem("acc2_saved")]
        masked = sem("masked")
        o_ready = sem("o_ready")
        sq_done, t_ready, x2_ready = sem("sq_done"), sem("t_ready"), sem("x2_ready")
        x2_stored, h_stored = sem("x2_stored"), sem("h_stored")
        dve_step = sem("dve_step")
        iotas_set, zeros_set = sem("iotas_set"), sem("zeros_set")
        w1_in, w2_in, b2_in, dump_in = sem("w1_in"), sem("w2_in"), sem("b2_in"), sem("dump_in")
        shifted, exped, chosen, counted = sem("logits_shifted"), sem("logits_exped"), sem("experts_chosen"), sem("tokens_counted")
        tags_ready, row_ready, row_used, listed = sem("tags_ready"), sem("row_ready"), sem("row_used"), sem("slots_listed")
        lists_ready, xgt_ones = sem("lists_ready"), sem("xgt_ones")
        xg_loaded = [sem(f"xg_loaded{i}") for i in range(2)]
        xgt_filled, xgt_ready, w1_staged = sem("xgt_filled"), sem("xgt_ready"), sem("w1_staged")
        hid_filled, hid_done, y_filled = sem("hid_filled"), sem("hid_done"), sem("y_filled")
        y_biased, y_weighted, scattered = sem("y_biased"), sem("y_weighted"), sem("scattered")

        def wait_filled(e, k):
            e.wait_ge(filled[k % RING], k // RING + 1)

        def wait_consumed(e, k):
            e.wait_ge(freed[k % RING], k // RING + 1)

        def segments(g):
            if g % GB == 1:
                return (0, 64, 0, 32), (1, 0, D // 2, 32)
            return ((0, 0, 0, 64),) if g % GB == 0 else ((1, 32, 0, 64),)

        def loads(g):
            return 16 * 2 * 3 * len(segments(g))

        def wait_past(e, s_, v):
            if not isinstance(v, int) or v > 0:
                e.wait_ge(s_, v)

        def over_blocks(eng, step):
            tail = 3
            step(0, 0)
            step(1, 1)
            with eng.Fori(1, (NBLK - tail) // 2) as pair:
                for i in range(2):
                    step(2 * pair + i, i)
            for j in range(NBLK - tail, NBLK):
                step(j, j % 2)

        with nc.Block() as block:

            @block.sync
            def _(sp):
                sp.dma_start(ids_sb[:, :].rearrange("p (b c) -> p b c", b=B),
                             ids.rearrange("b (p c) -> p b c", c=CT)).then_inc(ids_in, 16)
                sp.dma_start(scale_b[:, :], ln_scale.partition_broadcast(P)).then_inc(lnw_in, 16)
                sp.dma_start(bias_b[:, :], ln_bias.partition_broadcast(P)).then_inc(lnw_in, 16)
                sp.dma_start(WQKV[0:KW], qkv_wt.rearrange("(k p) m -> p k m", k=KC)).then_inc(wqkv_in, 16)
                sp.dma_start(WQKV[KW:KW + 1, 0, :], qkv_b.unsqueeze(0)).then_inc(wqkv_in, 16)
                sp.dma_start(PW[0:KW], proj_wt.rearrange("(k p) m -> p k m", k=KC)).then_inc(pw_in, 16)
                sp.dma_start(PW[KW:KW + 1, 0, :], proj_b.unsqueeze(0)).then_inc(pw_in, 16)
                sp.dma_start(PWN[0:KW], proj_wt_n.rearrange("(k p) m -> p k m", k=KC)).then_inc(pw_in, 16)
                sp.dma_start(PWN[KW:KW + 1, 0, :], proj_b_n.unsqueeze(0)).then_inc(pw_in, 16)
                sp.dma_start(GT[:, :, :], gate_wt.rearrange("(k p) e -> p k e", k=KC)).then_inc(gt_in, 16)

                def stack(g, dst, base, roles, done):
                    for r, nm in enumerate(roles):
                        for k, row, d0, n in segments(g):
                            sp.dma_start(dst[base + r * D + d0:base + r * D + d0 + n // GH, g % GB, :, :].bitcast(F32)
                                         .rearrange("d h n -> d (h n)"), QK[nm][row:row + n, k, :]).then_inc(done, 16)

                for kind, args in EVENTS:
                    if kind == "load_qk":
                        g, = args
                        sp.wait_ge(consts_set, 1)
                        wait_consumed(sp, unit("k_proj", g // GB))
                        wait_consumed(sp, unit("q_proj", g // GB))
                        if g >= GB:
                            wait_filled(sp, unit("exp_unit", g - GB, UG - 1))
                        stack(g, QS, 0, ("QH", "QH", "QL"), qk_loaded[g % GB])
                        stack(g, KS, 0, ("KH", "KL", "KH"), qk_loaded[g % GB])
                    elif kind == "max_row":
                        g, = args
                        wait_consumed(sp, unit("max_row", g))
                        for r, m in enumerate((MRH, MRL)):
                            sp.dma_start(QS[3 * D + r:3 * D + r + 1, g % GB, :, :].bitcast(F32).rearrange("o h n -> o (h n)"),
                                         m[:, g % 2, :].bitcast(F32)).then_inc(row_loaded[g % GB], 16)
                    elif kind == "load_sim":
                        g, = args
                        wait_consumed(sp, unit("t_transpose", g // GB))
                        if g >= GB:
                            wait_filled(sp, unit("sim_unit", g - GB, UG - 1))
                        stack(g, QS, 64, ("TH", "TH", "TL"), sim_loaded[g % GB])
                        stack(g, KS, 64, ("TH", "TL", "TH"), sim_loaded[g % GB])
                        if g == NG - 1:
                            sp.wait_ge(pv_done[0], 2 * NG)
                            for e in range(E):
                                sp.dma_start(w1_sb[0:KW, e], w1[e].rearrange("(k p) h -> p k h", k=KC)).then_inc(w1_in, 16)
                            sp.dma_start(w1_sb[KW:KW + 1, :, 0, :], b1.unsqueeze(0)).then_inc(w1_in, 16)
                            sp.wait_ge(zeros_set, 1)
                            sp.dma_start(out[DUMP:DUMP + P, :], zeros[:, :]).then_inc(dump_in, 16)
                    elif kind == "normalise" and args == (NG - 1, 1):
                        wait_filled(sp, unit("normalise", NG - 1, 1))
                        sp.wait_ge(pv_done[0], 2 * NG)
                        for e in range(E):
                            sp.dma_start(w2_sb[:, e], w2[e].rearrange("(k p) d -> p k d", p=P)).then_inc(w2_in, 16)
                    elif kind == "proj_out":
                        b, = args
                        sp.wait_ge(x2_ready, b + 1)
                        rows = slice(b * N, (b + 1) * N)
                        sp.dma_start(x2_rows[rows, :].rearrange("(p c) d -> p c d", c=CT), X2[:, :, :]).then_inc(x2_stored, 16)
                        sp.dma_start(out[rows, :].rearrange("(p c) d -> p c d", c=CT),
                                     H[:, CT * b:CT * (b + 1), :]).then_inc(h_stored, 16)
                sp.wait_ge(lists_ready, 1)
                sp.dma_start(b2_b, b2.partition_broadcast(P)).then_inc(b2_in, 16)
                sp.wait_ge(scattered, 16 * NBLK)

            @block.gpsimd
            def _(pool):
                pool.memset(ident[:, :], 0.0).then_inc(pool_step, 1)
                pool.wait_ge(pool_step, 1)
                pool.affine_select(out=ident[:, :], in_=ident[:, :], compare_op=ALU.not_equal, fill=1.0, base=0,
                                   pattern=[[-1, P]], channel_multiplier=1).then_inc(ident_set, 1)
                pool.wait_ge(rows_ready, 1)
                for t in range(TILES):
                    pool.indirect_dma_start(H[:, t, :], None, table,
                                            bass.IndirectOffsetOnAxis(ap=rows_sb[:, t:t + 1], axis=0)
                                            ).then_inc(gathered[t // CT], 16)
                any_dt = dict(allow_small_or_imprecise_dtypes=True)
                pool.memset(zeros[:, :], 0.0).then_inc(zeros_set, 1)
                pool.memset(ones[:, :], 1.0).then_inc(pool_step, 1)
                pool.memset(not_first[:, :, :], 1.0).then_inc(pool_step, 1)
                pool.iota(slot_no[:, :], pattern=[[1, P]], base=0, channel_multiplier=0, **any_dt)
                pool.iota(block_no[:, :], pattern=[[1, NBLK]], base=0, channel_multiplier=0, **any_dt)
                pool.iota(expert_no[:, :, :], pattern=[[0, TILES], [1, E]], base=0, channel_multiplier=0, **any_dt)
                pool.iota(token_1[:, :].rearrange("p (b c) -> p b c", b=B), pattern=[[N, B], [1, CT]], base=1,
                          channel_multiplier=CT, **any_dt)
                pool.iota(dump_1[:, :], pattern=[[0, 1]], base=DUMP + 1, channel_multiplier=1, **any_dt)
                pool.wait_ge(pool_step, 3)
                pool.affine_select(out=before[:, :], in_=ones[:, :], compare_op=ALU.is_gt, fill=0.0, base=0,
                                   pattern=[[1, P]], channel_multiplier=-1)
                pool.affine_select(out=not_first[:, :, :], in_=not_first[:, :, :], compare_op=ALU.is_gt, fill=0.0, base=0,
                                   pattern=[[0, E], [1, TILES]], channel_multiplier=0).then_inc(iotas_set, 1)
                step = 3
                for kind, args in EVENTS:
                    if kind == "embed_norm":
                        b, = args
                        h = H[:, CT * b:CT * (b + 1), :]
                        pool.wait_ge(normed_once, b + 1)
                        if b == 0:
                            pool.wait_ge(lnw_in, 32)
                        pool.tensor_tensor(h, h, scale_b[:, :].unsqueeze(1).to_broadcast([P, CT, C]), ALU.mult).then_inc(pool_step, 1)
                        step += 1
                        pool.wait_ge(pool_step, step)
                        pool.tensor_tensor(h, h, bias_b[:, :].unsqueeze(1).to_broadcast([P, CT, C]), ALU.add).then_inc(affine_done, 1)

                def gather(j):
                    if j >= 2:
                        pool.wait_ge(xgt_filled, j - 1)
                    pool.indirect_dma_start(XG[j % 2], None, x2_rows,
                                            bass.IndirectOffsetOnAxis(ap=slot_token[:, j:j + 1], axis=0)
                                            ).then_inc(xg_loaded[j % 2], 16)

                pool.wait_ge(lists_ready, 1)
                pool.wait_ge(x2_stored, 16 * B)
                for j in range(3):
                    gather(j)
                pool.wait_ge(h_stored, 16 * B)
                pool.wait_ge(dump_in, 16)
                for j in range(NBLK):
                    if j + 3 < NBLK:
                        gather(j + 3)
                    pool.wait_ge(y_weighted, j + 1)
                    if j >= 1:
                        pool.wait_ge(scattered, 16 * j)
                    pool.indirect_dma_start(out, bass.IndirectOffsetOnAxis(ap=slot_dest[:, j:j + 1], axis=0), Y[j % 2], None,
                                            compute_op=ALU.add).then_inc(scattered, 16)

            @block.scalar
            def _(act):
                for kind, args in EVENTS:
                    if kind not in PSUM_KINDS and kind != "pv":
                        continue
                    if kind == "pv":
                        g, u, ps = args
                        if u == 1:
                            act.wait_ge(pv_done[ps], 2 * g + 2)
                            if g >= 1:
                                wait_filled(act, unit("normalise", g - 1, ps))
                            act.activation(ACCS[:, ps, :], acc[ps], ACT.Copy).then_inc(acc_saved[ps], 1)
                        continue
                    k = unit(kind, *args)
                    done = freed[k % RING]
                    s = slot(k)
                    if kind == "x_transpose":
                        b, = args
                        wait_filled(act, k)
                        if b >= 1:
                            wait_filled(act, unit("v_proj", b - 1))
                        act.activation(XT[0:KW], s[0:KW], ACT.Copy).then_inc(done, 1)
                    elif kind in ("q_proj", "k_proj", "t_transpose"):
                        b, = args
                        wait_filled(act, k)
                        if b >= 1:
                            loaded = sim_loaded if kind == "t_transpose" else qk_loaded
                            for g in range(GB):
                                act.wait_ge(loaded[g], loads(g) * b)
                        nm = {"q_proj": "QH", "k_proj": "KH", "t_transpose": "TH"}[kind]
                        act.activation(QK[nm].bitcast(F32R), s[0:KW], ACT.Copy).then_inc(hi_written, 1)
                    elif kind == "v_proj":
                        b, = args
                        wait_filled(act, k)
                        act.activation(V[b][:, :, :, 0:D],
                                       slot4(k)[:, :, 0:C].rearrange("p c (h d) -> p c h d", d=D), ACT.Copy).then_inc(done, 1)
                    elif kind == "max_row":
                        g, = args
                        wait_filled(act, k)
                        if g >= 2:
                            act.wait_ge(row_loaded[(g - 2) % GB], 32 * ((g - 2) // GB + 1))
                        act.activation(MRH[:, g % 2, :], s[0:4 * GH, 0, 0:P], ACT.Copy, scale=-1.0).then_inc(hi_written, 1)
                    elif kind in ("exp_unit", "sim_unit"):
                        g, q = args
                        c = UG * g + q
                        ps = int(kind == "sim_unit")
                        wait_filled(act, k)
                        if c >= PRING:
                            act.wait_ge(pv_done[ps], (c - PRING) // GH + 1)
                        act.activation((P1, P2)[ps][:, c % PRING, :, :], s, ACT.Exp,
                                       scale=(QSCALE, SIM_SCALE)[ps]).then_inc(done, 1)
                    elif kind == "o_transpose":
                        b, ps = args
                        wait_filled(act, k)
                        if (b, ps) != (0, 0):
                            prev = [unit("proj_norm", b)] if ps else []
                            prev += [unit("proj_out", b - 1)] if b else []
                            prev += [unit("proj_norm", b + 1)] if ps and b + 1 < B and unit("proj_norm", b + 1) < k else []
                            prev = [p for p in prev if p < k]
                            for p in prev:
                                wait_filled(act, p)
                        act.activation(OT[0:KW], s[0:KW], ACT.Copy).then_inc(done, 1)
                    elif kind == "proj_norm":
                        wait_filled(act, k)
                        b, = args
                        if b >= 1:
                            wait_filled(act, unit("t_transpose", b - 1))
                        act.activation(T[:, :, :].rearrange("p (j c) d -> p j (c d)", j=2), s[:, :, 0:2 * C], ACT.Square).then_inc(sq_done, 1)
                    elif kind == "gate_transpose":
                        wait_filled(act, k)
                        act.activation(OT[0:KW], s[0:KW], ACT.Copy).then_inc(done, 1)

                act.wait_ge(shifted, 1)
                act.activation(rt["b"][:, :, :], rt["a"][:, :, :], ACT.Exp).then_inc(exped, 1)

                def step(j, i):
                    act.wait_ge(hid_filled, j + 1)
                    wait_past(act, y_filled, j - 1)
                    act.activation(HT[i].rearrange("p k t -> p (k t)"), hid_ps[i], ACT.Gelu).then_inc(hid_done, 1)

                over_blocks(act, step)

            @block.vector
            def _(dve):
                steps = [0]

                def link(ins):
                    steps[0] += 1
                    ins.then_inc(dve_step, 1)
                    dve.wait_ge(dve_step, steps[0])

                def rsqrt(dst, src, floor, add, n):
                    x, y, t = (nt[i][:, 0:n] for i in range(3))
                    link(dve.tensor_scalar(x, src, floor, add, ALU.max, ALU.add))
                    link(dve.tensor_scalar(t.bitcast(I32), x.bitcast(I32), 1, None, ALU.arith_shift_right))
                    link(dve.tensor_scalar(y.bitcast(I32), t.bitcast(I32), -1.0, float(RSQRT_MAGIC), ALU.mult, ALU.add))
                    for i in range(3):
                        link(dve.tensor_tensor(t, y, y, ALU.mult))
                        link(dve.scalar_tensor_tensor(t, t, -0.5, x, ALU.mult, ALU.mult))
                        link(dve.scalar_tensor_tensor(dst if i == 2 else y, t, 1.5, y, ALU.add, ALU.mult))

                def layer_norm(dst, src, eps, signal):
                    for c in range(CT):
                        last = dve.bn_stats(stats[:, c, :], src[:, c, :])
                    link(last)
                    for c in range(CT):
                        last = dve.bn_aggr(mv[:, c, :], stats[:, c, :])
                    link(last)
                    rstd = nt[3][:, 0:CT]
                    rsqrt(rstd, mv[:, :, 1], 0.0, eps, CT)
                    for c in range(CT):
                        last = dve.tensor_scalar(dst[:, c, :], src[:, c, :], mv[:, c, 0:1], rstd[:, c:c + 1],
                                                 ALU.subtract, ALU.mult)
                    last.then_inc(signal, 1)

                dve.wait_ge(ids_in, 16)
                dve.tensor_scalar(rows_sb[:, :], ids_sb[:, :], BUCKETS - 1, None, ALU.bitwise_and).then_inc(rows_ready, 1)
                dve.memset(XT[KW:KW + 1, 0, :], 1.0)
                dve.memset(OT[KW:KW + 1, 0, :], 1.0)
                dve.memset(KS[0:64, :, :, :].bitcast(F32), 1.0)
                dve.memset(acc[0], 0.0)
                dve.memset(acc[1], 0.0)
                for b in range(B):
                    last = dve.memset(V[b][:, :, :, D:VW], 1.0)
                last.then_inc(consts_set, 1)

                n_split = 0
                for kind, args in EVENTS:
                    k = unit(kind, *args) if kind in PSUM_KINDS else None
                    if kind == "embed_norm":
                        b, = args
                        h = H[:, CT * b:CT * (b + 1), :]
                        dve.wait_ge(gathered[b], 16 * CT)
                        layer_norm(h, h, 1e-6, normed_once)
                    elif kind == "attn_norm":
                        b, = args
                        dve.wait_ge(affine_done, b + 1)
                        if b >= 1:
                            wait_filled(dve, unit("x_transpose", b - 1))
                        layer_norm(X, H[:, CT * b:CT * (b + 1), :], 1e-5, x_ready)
                    elif kind in ("q_proj", "k_proj", "t_transpose"):
                        n_split += 1
                        dve.wait_ge(hi_written, n_split)
                        hi, lo = {"q_proj": ("QH", "QL"), "k_proj": ("KH", "KL"), "t_transpose": ("TH", "TL")}[kind]
                        dve.tensor_tensor(QK[lo].bitcast(F32R), slot(k)[0:KW], QK[hi],
                                          ALU.subtract).then_inc(freed[k % RING], 1)
                    elif kind == "max_unit":
                        g, q = args
                        i, u = q % GH, q // GH
                        if q == 0 and g >= 2:
                            wait_filled(dve, unit("max_row", g - 2))
                        wait_filled(dve, k)
                        dve.tensor_reduce(MX[:, g % 2, 4 * i + 2 * u:4 * i + 2 * u + 2], slot(k), AX_X, ALU.max
                                          ).then_inc(freed[k % RING], 1)
                    elif kind == "max_row":
                        g, = args
                        n_split += 1
                        dve.wait_ge(hi_written, n_split)
                        dve.scalar_tensor_tensor(MRL[:, g % 2, :], slot(k)[0:4 * GH, 0, 0:P], -1.0,
                                                 MRH[:, g % 2, :].bitcast(F32), ALU.mult, ALU.subtract
                                                 ).then_inc(freed[k % RING], 1)
                    elif kind == "mask":
                        g, q = args
                        wait_consumed(dve, unit("sim_unit", g, q))
                        p = P2[:, (UG * g + q) % PRING, :, :]
                        dve.scalar_tensor_tensor(p, p, 1.0, p, ALU.is_ge, ALU.mult).then_inc(masked, 1)
                    elif kind == "normalise":
                        g, ps = args
                        wait_filled(dve, k)
                        v = slot(k)[:, 0, :].rearrange("p (c h w) -> p c h w", c=CT, h=GH)
                        link(dve.reciprocal(rec[:, :, :], v[:, :, :, D]))
                        if g % GB == 0:
                            if g >= GB:
                                wait_filled(dve, unit("o_transpose", g // GB - 1, ps))
                        o = O[ps][:, :, (g % GB) * GH * D:(g % GB + 1) * GH * D].rearrange("p c (h d) -> p c h d", d=D)
                        dve.tensor_tensor(o, v[:, :, :, 0:D], rec[:, :, :].unsqueeze(3).to_broadcast([P, CT, GH, D]),
                                          ALU.mult).then_inc(freed[k % RING], 1)
                    elif kind == "proj_norm":
                        b, = args
                        dve.wait_ge(sq_done, b + 1)
                        ss = nt[3][:, 0:CT * NH]
                        tiles = T[:, :, :].rearrange("p c (g d h) -> p (c g) d h", g=GB, h=GH)
                        link(dve.tensor_reduce(ss, tiles.rearrange("p x d h -> p x h d"), AX_X, ALU.add))
                        rsqrt(ss, ss, 1e-24, 0.0, CT * NH)
                        scale = ss.rearrange("p (x h) -> p x h", h=GH)
                        for j in range(2):
                            x = slice(j * 2 * GB, (j + 1) * 2 * GB)
                            last = dve.tensor_tensor(tiles[:, x], slot(k)[:, j, 0:2 * C].rearrange("p (x d h) -> p x d h", d=D, h=GH),
                                                     scale[:, x].unsqueeze(2).to_broadcast([P, 2 * GB, D, GH]), ALU.mult)
                        last.then_inc(freed[k % RING], 1)
                    elif kind == "proj_out":
                        b, = args
                        h = H[:, CT * b:CT * (b + 1), :]
                        wait_filled(dve, k)
                        if b >= 1:
                            dve.wait_ge(x2_stored, 16 * b)
                            wait_filled(dve, unit("gate_transpose", b - 1))
                        dve.tensor_tensor(h, slot4(k)[:, :, 0:C], h, ALU.add).then_inc(freed[k % RING], 1)
                        wait_consumed(dve, k)
                        layer_norm(X2, h, 1e-5, x2_ready)
                    elif kind == "gate_logits":
                        b, = args
                        wait_filled(dve, k)
                        dve.tensor_copy(LG[:, CT * b:CT * (b + 1), :],
                                        slot(k)[:, 0, 0:CT * E].rearrange("p (c e) -> p c e", e=E)).then_inc(freed[k % RING], 1)

                def per_expert(v):
                    return v.unsqueeze(2).to_broadcast([P, TILES, E])

                a, bb, prob = rt["a"][:, :, :], rt["b"][:, :, :], rt["prob"][:, :, :]
                m, r = col["m"][:, :], col["r"][:, :]
                wait_consumed(dve, unit("gate_logits", B - 1))
                dve.wait_ge(iotas_set, 1)
                link(dve.tensor_reduce(m, LG[:, :, :], AX_X, ALU.max))
                dve.tensor_tensor(a, LG[:, :, :], per_expert(m), ALU.subtract).then_inc(shifted, 1)
                dve.wait_ge(exped, 1)
                link(dve.tensor_reduce(m, bb, AX_X, ALU.add))
                link(dve.reciprocal(r, m))
                link(dve.tensor_tensor(prob, bb, per_expert(r), ALU.mult))
                for n in range(TOPK):
                    top, oh = col[f"p{n}"][:, :], rt[f"oh{n}"][:, :, :]
                    link(dve.tensor_reduce(top, prob, AX_X, ALU.max))
                    link(dve.tensor_tensor(a, prob, per_expert(top), ALU.is_equal))
                    link(dve.scalar_tensor_tensor(a, a, -float(E), expert_no[:, :, :], ALU.mult, ALU.add))
                    link(dve.tensor_reduce(m, a, AX_X, ALU.min))
                    link(dve.tensor_tensor(oh, a, per_expert(m), ALU.is_equal))
                    if n == 0:
                        link(dve.scalar_tensor_tensor(prob, oh, -4.0, prob, ALU.mult, ALU.add))
                oh0, oh1 = rt["oh0"][:, :, :], rt["oh1"][:, :, :]
                dve.tensor_tensor(bb, oh0, oh1, ALU.add).then_inc(chosen, 1)
                link(dve.scalar_tensor_tensor(m, col["p0"][:, :], 1e-9, col["p1"][:, :], ALU.add, ALU.add))
                link(dve.reciprocal(r, m))
                for n in range(TOPK):
                    dve.tensor_tensor(weight[:, n, :], col[f"p{n}"][:, :], r, ALU.mult)
                dve.wait_ge(counted, 1)
                tot, inc = a.rearrange("p t e -> p (t e)").rearrange("p (e t) -> p e t", e=E), prob.rearrange("p t e -> p (t e)").rearrange("p (e t) -> p e t", e=E)
                link(dve.tensor_copy(tot, psum[:, 1, 0:P].rearrange("p (t e) -> p e t", e=E)))
                link(dve.tensor_tensor_scan(prob.rearrange("p t e -> p (t e)"), not_first[:, :, :].rearrange("p e t -> p (e t)"),
                                            a.rearrange("p t e -> p (t e)"), 0.0, ALU.mult, ALU.add))
                cnt, end, base = (exp8[nm][:, :] for nm in ("n", "end", "base"))
                link(dve.tensor_scalar(exp8_i[:, :], inc[:, :, TILES - 1], float(P - 1), None, ALU.add))
                link(dve.tensor_scalar(exp8_i[:, :], exp8_i[:, :], P.bit_length() - 1, None, ALU.arith_shift_right))
                link(dve.tensor_copy(cnt, exp8_i[:, :]))
                link(dve.tensor_tensor_scan(end, ones[:, 0:E], cnt, 0.0, ALU.mult, ALU.add))
                link(dve.tensor_tensor(base, end, cnt, ALU.subtract))
                link(dve.tensor_tensor(inc, inc, tot, ALU.subtract))
                link(dve.scalar_tensor_tensor(inc, base.unsqueeze(2).to_broadcast([P, E, TILES]), float(P), inc, ALU.mult, ALU.add))
                link(dve.tensor_tensor(bb, psum[:, 0, 0:P].rearrange("p (t e) -> p t e", e=E), inc.rearrange("p e t -> p t e"), ALU.add))
                for n in range(TOPK):
                    link(dve.tensor_tensor(a, bb, rt[f"oh{n}"][:, :, :], ALU.mult))
                    link(dve.tensor_reduce(place[:, n, :], a, AX_X, ALU.add))
                link(dve.tensor_copy(place_i[:, :, :], place[:, :, :]))
                link(dve.tensor_scalar(part_i[:, :, :], place_i[:, :, :], P - 1, None, ALU.bitwise_and))
                link(dve.tensor_copy(row_f[:, :, :], part_i[:, :, :]))
                link(dve.tensor_scalar(part_i[:, :, :], place_i[:, :, :], P.bit_length() - 1, None, ALU.arith_shift_right))
                link(dve.tensor_copy(blk_f[:, :, :], part_i[:, :, :]))
                blk = blk_f[:, :, :].rearrange("p n t -> p (n t)")
                link(dve.tensor_tensor(oh_blk, block_no[:, :].unsqueeze(1).to_broadcast([P, NQ, NBLK]),
                                       blk.unsqueeze(2).to_broadcast([P, NQ, NBLK]), ALU.is_equal))
                for n in range(TOPK):
                    dve.tensor_tensor(tag[:, n * TILES:(n + 1) * TILES, 0, :], oh_blk[:, n * TILES:(n + 1) * TILES, :],
                                      token_1[:, :].unsqueeze(2).to_broadcast([P, TILES, NBLK]), ALU.mult)
                dve.tensor_tensor(tag[:, :, 1, :], oh_blk, weight[:, :, :].rearrange("p n t -> p (n t)").unsqueeze(2).to_broadcast([P, NQ, NBLK]),
                                  ALU.mult).then_inc(tags_ready, 1)
                rows = row_f[:, :, :].rearrange("p n t -> p (n t)")
                for q in range(NQ):
                    if q >= OHR:
                        dve.wait_ge(row_used, q - OHR + 1)
                    dve.tensor_scalar(oh_row[:, q % OHR, :], slot_no[:, :], rows[:, q:q + 1], None, ALU.is_equal).then_inc(row_ready, 1)
                link(dve.tensor_tensor(blk_ge, block_no[0:1, :].unsqueeze(2).to_broadcast([1, NBLK, E]),
                                       end[0:1, :].unsqueeze(1).to_broadcast([1, NBLK, E]), ALU.is_ge))
                link(dve.tensor_reduce(blk_expert_f[:, :], blk_ge, AX_X, ALU.add))
                dve.tensor_scalar(blk_expert[:, :], blk_expert_f[:, :], float(E - 1), None, ALU.min)
                dve.wait_ge(listed, 1)
                tok = psum[:, 2, 0:NBLK]
                dve.tensor_copy(slot_weight[:, :], psum[:, 2, NBLK:2 * NBLK])
                dve.tensor_scalar(slot_token[:, :], tok, -1.0, 0.0, ALU.add, ALU.max)
                link(dve.tensor_scalar(slot_tmp[:, :], tok, 0.0, dump_1[:, 0:1], ALU.is_equal, ALU.mult))
                dve.scalar_tensor_tensor(slot_dest[:, :], tok, -1.0, slot_tmp[:, :], ALU.add, ALU.add).then_inc(lists_ready, 1)
                dve.wait_ge(lists_ready, 1)

                def stage(j, i):
                    e = dve.value_load(blk_expert[0:1, bass.ds(j, 1)], min_val=0, max_val=E - 1)
                    wait_past(dve, hid_filled, j - 1)
                    dve.tensor_copy(W1S[i][0:KW, 1, :], w1_sb[0:KW, bass.ds(e, 1), 1, :].rearrange("p o h -> p (o h)"))
                    dve.tensor_copy(W1S[i][0:KW + 1, 0, :], w1_sb[0:KW + 1, bass.ds(e, 1), 0, :].rearrange("p o h -> p (o h)")).then_inc(w1_staged, 1)

                def take_tokens(j, i):
                    dve.wait_ge(xgt_filled, j + 1)
                    dve.tensor_copy(XGT[i][0:KW, :, :], xgt_ps[i]).then_inc(xgt_ready, 1)

                def step(j, i):
                    if not isinstance(j, int) or j + 2 < NBLK:
                        stage(j + 2, i)
                        take_tokens(j + 2, i)
                    e = dve.value_load(blk_expert[0:1, bass.ds(j, 1)], min_val=0, max_val=E - 1)
                    dve.wait_ge(y_filled, j + 1)
                    wait_past(dve, scattered, 16 * (j - 1))
                    dve.tensor_tensor(Y[i], y_ps[i], b2_b[:, bass.ds(e, 1), :].rearrange("p o d -> p (o d)"), ALU.add).then_inc(y_biased, 1)
                    dve.wait_ge(y_biased, j + 1)
                    dve.tensor_scalar(Y[i], Y[i], slot_weight[:, bass.ds(j, 1)], None, ALU.mult).then_inc(y_weighted, 1)

                dve.wait_ge(w1_in, 16 * (E + 1))
                for j in range(2):
                    stage(j, j)
                    take_tokens(j, j)
                dve.wait_ge(b2_in, 16)
                over_blocks(dve, step)

            @block.tensor
            def _(pe):
                pe.wait_ge(ident_set, 1)
                for kind, args in EVENTS:
                    if kind == "pv":
                        g, u, ps = args
                        b = g // GB
                        if ps == 0:
                            for q in range(GH * u, GH * u + GH):
                                wait_consumed(pe, unit("exp_unit", g, q))
                            wait_consumed(pe, unit("v_proj", b))
                        else:
                            pe.wait_ge(masked, UG * g + GH * (u + 1))
                        if u == 0 and g >= 1:
                            pe.wait_ge(acc_saved[ps], g)
                        for j in range(2):
                            for i in range(GH):
                                c = UG * g + GH * u + i
                                last = pe.matmul(acc[ps][32 * i:32 * i + VW, :], V[b][:, 2 * u + j, GH * (g % GB) + i, :],
                                                 (P1, P2)[ps][:, c % PRING, j, :], start=(u == 0 and j == 0),
                                                 stop=(u == 1 and j == 1))
                        last.then_inc(pv_done[ps], 1)
                        continue
                    if kind not in PSUM_KINDS:
                        continue
                    k = unit(kind, *args)
                    s = slot(k)
                    if k >= RING:
                        wait_consumed(pe, k - RING)
                    if kind in ("x_transpose", "t_transpose", "o_transpose", "gate_transpose"):
                        b = args[0]
                        src = O[args[1]] if kind == "o_transpose" else {"x_transpose": X, "t_transpose": T, "gate_transpose": X2}[kind]
                        if kind == "x_transpose":
                            pe.wait_ge(x_ready, b + 1)
                        elif kind == "gate_transpose":
                            pe.wait_ge(x2_ready, b + 1)
                        elif kind == "t_transpose":
                            wait_consumed(pe, unit("proj_norm", b))
                        else:
                            for g in range(GB * b, GB * b + GB):
                                wait_consumed(pe, unit("normalise", g, args[1]))
                        for kc in range(KC):
                            for c in range(CT):
                                last = pe.transpose(s[0:KW, kc, c * P:(c + 1) * P], src[:, c, kc * KW:(kc + 1) * KW], ident[:, :])
                    elif kind in ("q_proj", "k_proj"):
                        b, = args
                        m0 = C * (kind == "k_proj")
                        wait_consumed(pe, unit("x_transpose", b))
                        if b == 0:
                            pe.wait_ge(wqkv_in, 32)
                            pe.wait_ge(consts_set, 1)
                        for m in range(KC):
                            for kc in range(KC):
                                rows = KW + (kc == 0)
                                last = pe.matmul(s[0:KW, m, :], WQKV[0:rows, kc, m0 + m * KW:m0 + (m + 1) * KW],
                                                 XT[0:rows, kc, :], start=kc == 0, stop=kc == KC - 1)
                    elif kind == "v_proj":
                        b, = args
                        wait_consumed(pe, unit("x_transpose", b))
                        for c in range(CT):
                            for kc in range(KC):
                                rows = KW + (kc == 0)
                                last = pe.matmul(slot4(k)[:, c, 0:C], XT[0:rows, kc, c * P:(c + 1) * P],
                                                 WQKV[0:rows, kc, 2 * C:3 * C], start=kc == 0, stop=kc == KC - 1)
                    elif kind == "max_unit":
                        g, q = args
                        i, u, sl = q % GH, q // GH, g % GB
                        if q == 0:
                            pe.wait_ge(qk_loaded[sl], loads(g) * (g // GB + 1))
                        for j in range(2):
                            c = 2 * u + j
                            last = pe.matmul(s[:, j, :], QS[0:3 * D, sl, i, c * P:(c + 1) * P], KS[0:3 * D, sl, i, :],
                                             start=True, stop=True)
                    elif kind == "exp_unit":
                        g, q = args
                        i, u, sl = q % GH, q // GH, g % GB
                        if q == 0:
                            pe.wait_ge(row_loaded[sl], 32 * (g // GB + 1))
                        for j in range(2):
                            c = 2 * u + j
                            last = pe.matmul(s[:, j, :], KS[0:3 * D + 2, sl, i, c * P:(c + 1) * P], QS[0:3 * D + 2, sl, i, :],
                                             start=True, stop=True)
                    elif kind == "sim_unit":
                        g, q = args
                        i, u, sl = q % GH, q // GH, g % GB
                        if q == 0:
                            pe.wait_ge(sim_loaded[sl], loads(g) * (g // GB + 1))
                        for j in range(2):
                            c = 2 * u + j
                            last = pe.matmul(s[:, j, :], QS[64:64 + 3 * D, sl, i, c * P:(c + 1) * P],
                                             KS[64:64 + 3 * D, sl, i, :], start=True, stop=True)
                    elif kind == "max_row":
                        g, = args
                        pe.wait_ge(freed[unit("max_unit", g, UG - 1) % RING], unit("max_unit", g, UG - 1) // RING + 1)
                        wait_consumed(pe, unit("max_unit", g, UG - 2))
                        last = pe.transpose(s[0:4 * GH, 0, 0:P], MX[:, g % 2, :], ident[:, :])
                    elif kind == "normalise":
                        g, ps = args
                        pe.wait_ge(acc_saved[ps], g + 1)
                        for c in range(CT):
                            last = pe.transpose(s[:, 0, c * P:(c + 1) * P], ACCS[:, ps, c * P:(c + 1) * P], ident[:, :])
                    elif kind in ("proj_norm", "proj_out"):
                        b, = args
                        norm = kind == "proj_norm"
                        wait_consumed(pe, unit("o_transpose", b, int(not norm)))
                        if b == 0:
                            pe.wait_ge(pw_in, 64)
                        for c in range(CT):
                            for kc in range(KC):
                                rows = KW + (kc == 0)
                                last = pe.matmul(slot2(k, c) if norm else slot4(k)[:, c, 0:C], OT[0:rows, kc, c * P:(c + 1) * P],
                                                 (PWN if norm else PW)[0:rows, kc, :],
                                                 start=kc == 0, stop=kc == KC - 1)
                    elif kind == "gate_logits":
                        b, = args
                        wait_consumed(pe, unit("gate_transpose", b))
                        if b == 0:
                            pe.wait_ge(gt_in, 16)
                        for c in range(CT):
                            for kc in range(KC):
                                last = pe.matmul(s[:, 0, c * E:(c + 1) * E], OT[0:KW, kc, c * P:(c + 1) * P], GT[:, kc, :],
                                                 start=kc == 0, stop=kc == KC - 1)
                    last.then_inc(filled[k % RING], 1)

                chose = rt["b"][:, :, :].rearrange("p t e -> p (t e)")
                pe.wait_ge(chosen, 1)
                pe.wait_ge(iotas_set, 1)
                pe.matmul(psum[:, 0, 0:P], before[:, :], chose, start=True, stop=True)
                pe.matmul(psum[:, 1, 0:P], ones[:, :], chose, start=True, stop=True).then_inc(counted, 1)
                pe.wait_ge(tags_ready, 1)
                for q in range(NQ):
                    pe.wait_ge(row_ready, q + 1)
                    last = pe.matmul(psum[:, 2, 0:2 * NBLK], oh_row[:, q % OHR, :], tag[:, q, :, :].rearrange("p s j -> p (s j)"),
                                     start=q == 0, stop=q == NQ - 1)
                    last.then_inc(row_used if q < NQ - 1 else listed, 1)

                def turn(j, i):
                    pe.wait_ge(xg_loaded[i], 8 * (j + 2 - i))
                    wait_past(pe, xgt_ready, j - 1)
                    for kc in range(KC):
                        last = pe.transpose(xgt_ps[i][:, kc, :], XG[i][:, kc * KW:(kc + 1) * KW], ident[:, :])
                    last.then_inc(xgt_filled, 1)

                def first_layer(j, i):
                    pe.wait_ge(xgt_ready, j + 1)
                    pe.wait_ge(w1_staged, j + 1)
                    wait_past(pe, hid_done, j - 1)
                    for hc in range(HC):
                        for kc in range(KC):
                            rows = KW + (kc == 0)
                            last = pe.matmul(hid_ps[i][:, hc * P:(hc + 1) * P], W1S[i][0:rows, kc, hc * P:(hc + 1) * P],
                                             XGT[i][0:rows, kc, :], start=kc == 0, stop=kc == KC - 1)
                    last.then_inc(hid_filled, 1)

                def second_layer(j, i):
                    e = pe.value_load(blk_expert[0:1, bass.ds(j, 1)], min_val=0, max_val=E - 1)
                    pe.wait_ge(hid_done, j + 1)
                    wait_past(pe, y_weighted, j - 1)
                    for hc in range(HC):
                        last = pe.matmul(y_ps[i], HT[i][:, hc, :], w2_sb[:, bass.ds(e, 1), hc, :].rearrange("p o d -> p (o d)"),
                                         start=hc == 0, stop=hc == HC - 1)
                    last.then_inc(y_filled, 1)

                def step(j, i):
                    if not isinstance(j, int) or j + 2 < NBLK:
                        turn(j + 2, i)
                    if not isinstance(j, int) or j + 1 < NBLK:
                        first_layer(j + 1, (i + 1) % 2)
                    second_layer(j, i)

                pe.wait_ge(lists_ready, 1)
                turn(0, 0)
                turn(1, 1)
                first_layer(0, 0)
                pe.wait_ge(w2_in, 16 * E)
                over_blocks(pe, step)


def kernel(x, L0_tok_tables, L0_tok_ln_scale, L0_tok_ln_bias, L0_attn_qkv_w, L0_attn_qkv_b, L0_attn_proj_w,
           L0_attn_proj_b, L0_ffn_gate_w, L0_ffn_w1, L0_ffn_b1, L0_ffn_w2, L0_ffn_b2):
    import numpy as np
    import concourse.bacc as bacc
    from concourse.bass_utils import run_bass_kernel_spmd

    primes = (31, 43, 59, 61, 73, 97, 103, 113)
    r = np.arange(BUCKETS)
    tables = np.asarray(L0_tok_tables)
    table = np.concatenate([tables[h][(r + 1) * p % BUCKETS] for h, p in enumerate(primes)], axis=1)
    by_width = np.arange(C).reshape(GB, GH, D).transpose(0, 2, 1).reshape(-1)
    qkv_cols = np.concatenate([by_width, C + by_width, 2 * C + np.arange(C)])
    proj_wt = np.asarray(L0_attn_proj_w).T
    arrays = {
        "ids": np.asarray(x), "table": table, "ln_scale": L0_tok_ln_scale, "ln_bias": L0_tok_ln_bias,
        "qkv_wt": np.asarray(L0_attn_qkv_w).T[:, qkv_cols], "qkv_b": np.asarray(L0_attn_qkv_b)[qkv_cols],
        "proj_wt": proj_wt, "proj_b": L0_attn_proj_b,
        "proj_wt_n": proj_wt[:, by_width], "proj_b_n": np.asarray(L0_attn_proj_b)[by_width],
        "gate_wt": np.asarray(L0_ffn_gate_w).T, "w1": L0_ffn_w1, "b1": L0_ffn_b1, "w2": L0_ffn_w2, "b2": L0_ffn_b2,
    }
    arrays = {k: np.ascontiguousarray(v) for k, v in arrays.items()}
    nc = bacc.Bacc("TRN2", target_bir_lowering=False, num_devices=1)
    args = [nc.dram_tensor(k, a.shape, mybir.dt.from_np(a.dtype), kind="ExternalInput").ap() for k, a in arrays.items()]
    result = nc.dram_tensor("result", (B * N + P, C), F32, kind="ExternalOutput").ap()
    build(nc, *args, result)
    r = run_bass_kernel_spmd(nc, [arrays], core_ids=[0])
    return r.results[0]["result"][:B * N].reshape(B, N, C)
```

```python
from contextlib import ExitStack

import concourse.bass as bass
from concourse import mybir

F32 = mybir.dt.float32
BF16 = mybir.dt.bfloat16
I32 = mybir.dt.int32
U32 = mybir.dt.uint32
ALU = mybir.AluOpType
ACT = mybir.ActivationFunctionType
AX_X = mybir.AxisListType.X

P = 128
B, N, C = 4, 512, 192
NH, D = 12, 16
BUCKETS = 4096
CT = N // P
TILES = B * CT
KC, KW = 2, 96
GH = 4
GB = NH // GH
NG = B * GB
GC = GH * D
Q_PARTS, K_PARTS = "HMHMHL", "HHMMLH"
SD = len(Q_PARTS) * D
SLOTS = (4, 2)
UG = 2 * GH
VW = D + 1
E, HID = 8, 768
HC = HID // P
TOPK = 2
NBLK = (B * N * TOPK) // P + E - 1
DUMP = B * N
QSCALE = D ** -0.5
SIM_SCALE = 10.0
RING = 6
PRING = 6
RSQRT_MAGIC = 0x5F3759DF

OFF_C, OFF_E = 11, 52


def schedule():
    ev = []

    def at(t, rank, kind, *args):
        ev.append((t, rank, kind, args))

    for b in range(B):
        a = GB * UG * b
        first = b == 0
        if first:
            at(-9, 0, "embed_norm", 0, 1)
            at(-3, 1, "embed_norm", 1, B)
            at(1, 1, "attn_stats", 1, B)
        at(-8 if first else a - 21, 0, "attn_norm", b)
        for j in range(2):
            h = j / 2
            at(-7 + h if first else a - 17 + h, 0, "x_transpose", b, j)
            at(-6 + h if first else a - 15 + j, 0, "q_proj", b, j)
            at(-5 + h if first else a - 14.5 + j, 0, "k_proj", b, j)
            at(-5 + h if first else a - 14 + j, 1, "mid", "q_proj", b, j)
            at(-4 + h if first else a - 12.5 + j, 0, "v_proj", b, j)
            at(-4 + h if first else a - 13.5 + j, 1, "mid", "k_proj", b, j)
        d = a + GB * UG - UG + OFF_C + UG + 3
        f = a + GB * UG - UG + OFF_E + UG + 4
        for j in range(2):
            h = j / 2
            at(d + h, 6, "o_transpose", b, 0, j)
            at(d + 1.5 + h, 6, "proj_norm", b, j)
            at(d + 5 + h, 6, "t_transpose", b, j)
            at(d + 6 + h, 6, "mid", "t_transpose", b, j)
            at(f + h, 6, "o_transpose", b, 1, j)
            at(f + 2 + h, 6, "proj_out", b, j)
            at(f + 8.5 + h, 6, "gate_transpose", b, j)
        at(d + 4, 6, "unit_tokens", b)
        at(f + 3, 6, "out_norm", b)
        at(f + 10, 6, "gate_logits", b)
    for g in range(NG):
        a = UG * g
        at(-3 + g % GB if g < GB else a - (10 if g % GB else 8), 1, "load_qk", g)
        for q in range(UG):
            for j in range(2):
                at(a + q + j / 2, 2, "max_unit", g, q, j)
                at(a + OFF_C + q + j / 2, 3, "exp_unit", g, q, j)
                at(a + OFF_E + q + j / 2, 4, "sim_unit", g, q, j)
            at(a + OFF_E + q + 1, 0, "mask", g, q)
        at(a + UG, 5, "max_row", g)
        for u in range(2):
            for j in range(2):
                at(a + OFF_C + 4.5 + 4 * u + j / 2, 5, "pv", g, u, j, 0)
                at(a + OFF_E + 5 + 4 * u + j / 2, 5, "pv", g, u, j, 1)
        at(a + OFF_C + UG + 3, 5, "normalise", g, 0)
        at(a + OFF_E + UG + 4, 5, "normalise", g, 1)
        b = g // GB
        ready = GB * UG * b + GB * UG - UG + OFF_C + UG + 3 + 6
        at(max(ready + 1, a + OFF_E - 8), 7, "load_sim", g)
    ev.sort(key=lambda e: (e[0], e[1]))
    return [(kind, args) for _, _, kind, args in ev]


EVENTS = schedule()
PSUM_KINDS = ("x_transpose", "q_proj", "k_proj", "v_proj", "max_unit", "max_row", "exp_unit", "normalise",
              "o_transpose", "proj_norm", "t_transpose", "sim_unit", "proj_out", "gate_transpose", "gate_logits")
UNIT = {ev: k for k, ev in enumerate(e for e in EVENTS if e[0] in PSUM_KINDS)}


SPLIT = {ev: k for k, ev in enumerate(e for e in EVENTS if e[0] in ("q_proj", "k_proj", "t_transpose"))}


def unit(kind, *args):
    return UNIT[(kind, args)]


def build(nc, ids, table, ln_scale, ln_bias, qkv_wt, qkv_b, proj_wt, proj_b, proj_wt_n, proj_b_n, gate_wt, w1, b1, w2, b2, out):
    ctx = ExitStack()
    with ctx:
        def sb(name, shape, dt=F32):
            return ctx.enter_context(nc.sbuf_tensor(name, shape, dt))

        def sem(name):
            return ctx.enter_context(nc.semaphore(name))

        x2_rows = nc.dram_tensor("x2_rows", (B * N, C), F32).ap()

        ident = sb("ident", [P, P])
        ids_sb = sb("ids_sb", [P, TILES], I32)
        rows_sb = sb("rows_sb", [P, TILES], I32)
        H = sb("H", [P, TILES, C])
        X = sb("X", [P, CT, C])
        X2 = sb("X2", [P, CT, C])
        scale_b = sb("scale_b", [P, C])
        bias_b = sb("bias_b", [P, C])
        stats = sb("stats", [P, TILES, 6])
        mv = sb("mv", [P, TILES, 2])
        mv_x = sb("mv_x", [P, TILES, 2])
        rstd_x = sb("rstd_x", [P, TILES])
        nt = [sb(f"newton{i}", [P, CT * NH]) for i in range(4)]
        LG = sb("LG", [P, TILES, E])

        W1B = E * KC * HID
        arena1 = sb("arena1", [P, W1B])
        w1_sb = arena1[:, :].rearrange("p (e k h) -> p e k h", e=E, k=KC)
        at1 = [0]

        def carve(arena, pos, free):
            v = arena[:, pos[0]:pos[0] + free]
            pos[0] += free
            return v

        P1 = carve(arena1, at1, PRING * 2 * N).rearrange("p (s j n) -> p s j n", s=PRING, j=2)
        XT = carve(arena1, at1, KC * N).rearrange("p (k n) -> p k n", k=KC)
        WQKV = carve(arena1, at1, KC * 3 * C).rearrange("p (k m) -> p k m", k=KC)
        assert at1[0] <= W1B
        PART = KC * N // 2
        arena3 = sb("arena3", [P, 9 * PART + 2 * KC * N])
        PARTS = {nm: arena3[:, i * PART:(i + 1) * PART].bitcast(BF16).rearrange("p (k n) -> p k n", k=KC)
                 for i, nm in enumerate(r + part for r in "QKT" for part in "HML")}
        RESTS = 2 * KC
        REST = [arena3[:, 9 * PART + i * N:9 * PART + (i + 1) * N] for i in range(RESTS)]
        QS = [[carve(arena1, at1, GH * N // 2)[0:SD + 2].bitcast(BF16).rearrange("p (h n) -> p h n", h=GH) if i < 3
               else sb(f"QS0_{i}", [SD + 2, GH, N], BF16)[:, :, :] for i in range(SLOTS[0])],
              [sb(f"QS1_{i}", [SD, GH, N], BF16)[:, :, :] for i in range(SLOTS[1])]]
        KS = [[sb(f"KS{ps}_{i}", [SD + 2 * (ps == 0), GH, N], BF16)[:, :, :] for i in range(SLOTS[ps])] for ps in range(2)]
        assert at1[0] <= W1B
        w2_free = E * HC * C
        arena2 = sb("arena2", [P, B * CT * NH * VW + PRING * 2 * N + 2 * N])
        w2_sb = arena2[:, 0:w2_free].rearrange("p (e k d) -> p e k d", e=E, k=HC)
        at2 = [0]
        V = [carve(arena2, at2, CT * NH * VW).rearrange("p (c h w) -> p c h w", c=CT, h=NH) for _ in range(B)]
        P2 = carve(arena2, at2, PRING * 2 * N).rearrange("p (s j n) -> p s j n", s=PRING, j=2)
        ACCS = carve(arena2, at2, 2 * N).rearrange("p (s n) -> p s n", s=2)
        O = [sb(f"O{ps}", [P, CT, C]) for ps in range(2)]
        OT = sb("OT", [KW + 1, KC, N])
        T = sb("T", [P, CT, C])
        SQ = sb("SQ", [P, CT, C])
        PW = sb("PW", [KW + 1, KC, C])
        PWN = sb("PWN", [KW + 1, KC, C])
        GT = sb("GT", [KW, KC, E])
        MX = sb("MX", [P, 2, 4 * GH])
        MRH = sb("MRH", [4 * GH, 2, P], BF16)
        MRM = sb("MRM", [4 * GH, 2, P], BF16)
        rec = sb("rec", [P, CT, GH])

        x_flat, x_at = X[:, :, :].rearrange("p c d -> p (c d)"), [0]

        zeros = sb("zeros", [P, C])
        ones = sb("ones", [P, P])
        before = sb("before", [P, P])
        slot_no = sb("slot_no", [P, P])
        block_no = sb("block_no", [P, NBLK])
        expert_no = sb("expert_no", [P, TILES, E])
        not_first = sb("not_first", [P, E, TILES])
        token_1 = sb("token_1", [P, TILES])
        dump_1 = sb("dump_1", [P, 1])
        rt = {nm: sb(f"rt_{nm}", [P, TILES, E]) for nm in ("a", "b", "oh0", "oh1", "prob")}
        col = {nm: sb(f"col_{nm}", [P, TILES]) for nm in ("m", "p0", "p1", "r")}
        weight = sb("weight", [P, TOPK, TILES])
        place = carve(x_flat, x_at, TOPK * TILES).rearrange("p (k t) -> p k t", k=TOPK)
        place_i = sb("place_i", [P, TOPK, TILES], I32)
        part_i = sb("part_i", [P, TOPK, TILES], I32)
        row_f = carve(x_flat, x_at, TOPK * TILES).rearrange("p (k t) -> p k t", k=TOPK)
        blk_f = carve(x_flat, x_at, TOPK * TILES).rearrange("p (k t) -> p k t", k=TOPK)
        exp8 = {nm: sb(f"exp8_{nm}", [P, E]) for nm in ("n", "end", "base")}
        exp8_i = sb("exp8_i", [P, E], I32)
        NQ = TOPK * TILES
        oh_blk = arena3[:, 0:NQ * NBLK].rearrange("p (q j) -> p q j", j=NBLK)
        tag = arena3[:, NQ * NBLK:3 * NQ * NBLK].rearrange("p (q s j) -> p q s j", s=2, j=NBLK)
        OHR = 8
        oh_row = arena3[:, 3 * NQ * NBLK:3 * NQ * NBLK + OHR * P].rearrange("p (s r) -> p s r", s=OHR)
        assert 3 * NQ * NBLK + OHR * P <= 9 * PART + 2 * KC * N
        slot_token = sb("slot_token", [P, NBLK], I32)
        slot_dest = sb("slot_dest", [P, NBLK], I32)
        slot_weight = carve(x_flat, x_at, NBLK)
        slot_tmp = carve(x_flat, x_at, NBLK)
        blk_ge = carve(x_flat, x_at, NBLK * E)[0:1, :].rearrange("p (j e) -> p j e", e=E)
        blk_expert_f = carve(x_flat, x_at, NBLK)[0:1, :]
        blk_expert = sb("blk_expert", [1, NBLK], I32)
        at3 = [0]
        W1S = [carve(arena3, at3, KC * HID).rearrange("p (k h) -> p k h", k=KC) for _ in range(2)]
        HT = [carve(arena3, at3, HID).rearrange("p (k t) -> p k t", k=HC) for _ in range(2)]
        b2_b = carve(arena3, at3, E * C).rearrange("p (e d) -> p e d", e=E)
        XG = [T[:, i, :] for i in range(2)]
        XGT = [OT[:, :, i * P:(i + 1) * P] for i in range(2)]
        Y = [T[:, 2 + i, :] for i in range(2)]

        psum = ctx.enter_context(nc.psum_tensor("psum", [P, 8, N], F32))
        acc = [psum[:, 6, :], psum[:, 7, :]]

        def slot(k):
            return psum[:, k % RING, :]

        def slot_tiles(k):
            return psum[:, k % RING, 0:2 * C].rearrange("p (c d) -> p c d", c=2)

        hid_ps = [psum[:, 2 * i:2 * i + 2, :].rearrange("p b n -> p (b n)")[:, 0:HID] for i in range(2)]
        xgt_ps = [psum[0:KW, 4 + i, 0:KC * P].rearrange("p (k t) -> p k t", k=KC) for i in range(2)]
        y_ps = [psum[:, 6 + i, 0:C] for i in range(2)]

        ids_in, lnw_in, wqkv_in, pw_in, gt_in = (sem(s) for s in ("ids_in", "lnw_in", "wqkv_in", "pw_in", "gt_in"))
        ident_set, consts_set, ones_set, rows_ready = (sem(x) for x in ("ident_set", "consts_set", "ones_set", "rows_ready"))
        gathered = [sem(f"gathered{b}") for b in range(B)]
        filled = [sem(f"psum_filled{s}") for s in range(RING)]
        freed = [sem(f"psum_freed{s}") for s in range(RING)]
        hi_written, mid_written, lo_written, row_hi = (sem(x) for x in ("hi_written", "mid_written", "lo_written", "row_hi"))
        x_ready = sem("x_ready")
        pool_step = sem("pool_step")
        max_done = sem("max_done")
        qk_loaded = {x: [sem(f"{x}_loaded{s}") for s in range(SLOTS[0])] for x in "qk"}
        row_loaded = [sem(f"row_loaded{s}") for s in range(SLOTS[0])]
        sim_loaded = {x: [sem(f"sim_{x}_loaded{s}") for s in range(SLOTS[1])] for x in "qk"}
        pv_done = [sem("pv1_done"), sem("pv2_done")]
        acc_saved = [sem("acc1_saved"), sem("acc2_saved")]
        masked = sem("masked")
        o_ready = sem("o_ready")
        sq_done, t_ready, x2_ready = sem("sq_done"), sem("t_ready"), sem("x2_ready")
        x2_stored, h_stored = sem("x2_stored"), sem("h_stored")
        dve_step = sem("dve_step")
        iotas_set, zeros_set = sem("iotas_set"), sem("zeros_set")
        w1_in, w2_in, b2_in, dump_in = sem("w1_in"), sem("w2_in"), sem("b2_in"), sem("dump_in")
        shifted, exped, chosen, counted = sem("logits_shifted"), sem("logits_exped"), sem("experts_chosen"), sem("tokens_counted")
        tags_ready, row_ready, row_used, listed = sem("tags_ready"), sem("row_ready"), sem("row_used"), sem("slots_listed")
        lists_ready, xgt_ones = sem("lists_ready"), sem("xgt_ones")
        xg_loaded = [sem(f"xg_loaded{i}") for i in range(2)]
        xgt_filled, xgt_ready, w1_staged = sem("xgt_filled"), sem("xgt_ready"), sem("w1_staged")
        hid_filled, hid_done, y_filled = sem("hid_filled"), sem("hid_done"), sem("y_filled")
        y_biased, y_weighted, scattered = sem("y_biased"), sem("y_weighted"), sem("scattered")

        def wait_filled(e, k):
            e.wait_ge(filled[k % RING], k // RING + 1)

        def wait_consumed(e, k):
            e.wait_ge(freed[k % RING], k // RING + 1)

        def part_rows(nm, g):
            return PARTS[nm][GC * (g % 2):GC * (g % 2) + GC, 0, :] if g < 2 else PARTS[nm][GC:2 * GC, 1, :]

        LOADS = 16 * len(Q_PARTS)

        def stack(eng, g, ps, dst, role, parts, done):
            for r, part in enumerate(parts):
                eng.dma_start(dst[g % SLOTS[ps]][r * D:(r + 1) * D, :, :].rearrange("d h n -> d (h n)"),
                              part_rows(role + part, g % GB)).then_inc(done, 16)

        def load_qk(eng, g, dst, role, parts):
            eng.wait_ge(lo_written, SPLIT[({"Q": "q_proj", "K": "k_proj"}[role], (g // GB, 1))] + 1)
            if g >= SLOTS[0]:
                wait_filled(eng, unit("exp_unit", g - SLOTS[0], UG - 1, 1))
            stack(eng, g, 0, dst, role, parts, qk_loaded[role.lower()][g % SLOTS[0]])

        def load_sim(eng, g, dst, side, parts):
            eng.wait_ge(lo_written, SPLIT[("t_transpose", (g // GB, 1))] + 1)
            if g >= SLOTS[1]:
                wait_filled(eng, unit("sim_unit", g - SLOTS[1], UG - 1, 1))
            stack(eng, g, 1, dst, "T", parts, sim_loaded[side][g % SLOTS[1]])

        def wait_past(e, s_, v):
            if not isinstance(v, int) or v > 0:
                e.wait_ge(s_, v)

        def over_blocks(eng, step):
            tail = 3
            step(0, 0)
            step(1, 1)
            with eng.Fori(1, (NBLK - tail) // 2) as pair:
                for i in range(2):
                    step(2 * pair + i, i)
            for j in range(NBLK - tail, NBLK):
                step(j, j % 2)

        with nc.Block() as block:

            @block.sync
            def _(sp):
                sp.dma_start(ids_sb[:, :].rearrange("p (b c) -> p b c", b=B),
                             ids.rearrange("b (p c) -> p b c", c=CT)).then_inc(ids_in, 16)
                sp.dma_start(scale_b[:, :], ln_scale.partition_broadcast(P)).then_inc(lnw_in, 16)
                sp.dma_start(bias_b[:, :], ln_bias.partition_broadcast(P)).then_inc(lnw_in, 16)
                sp.dma_start(WQKV[0:KW], qkv_wt.rearrange("(k p) m -> p k m", k=KC)).then_inc(wqkv_in, 16)
                sp.dma_start(WQKV[KW:KW + 1, 0, :], qkv_b.unsqueeze(0)).then_inc(wqkv_in, 16)
                sp.dma_start(PW[0:KW], proj_wt.rearrange("(k p) m -> p k m", k=KC)).then_inc(pw_in, 16)
                sp.dma_start(PW[KW:KW + 1, 0, :], proj_b.unsqueeze(0)).then_inc(pw_in, 16)
                sp.dma_start(PWN[0:KW], proj_wt_n.rearrange("(k p) m -> p k m", k=KC)).then_inc(pw_in, 16)
                sp.dma_start(PWN[KW:KW + 1, 0, :], proj_b_n.unsqueeze(0)).then_inc(pw_in, 16)
                sp.dma_start(GT[:, :, :], gate_wt.rearrange("(k p) e -> p k e", k=KC)).then_inc(gt_in, 16)

                for kind, args in EVENTS:
                    if kind == "load_qk":
                        g, = args
                        load_qk(sp, g, QS[0], "Q", Q_PARTS)
                    elif kind == "max_row":
                        g, = args
                        wait_consumed(sp, unit("max_row", g))
                        for r, m in enumerate((MRH, MRM)):
                            sp.dma_start(QS[0][g % SLOTS[0]][SD + r:SD + r + 1, :, :].rearrange("o h n -> o (h n)"),
                                         m[:, g % 2, :]).then_inc(row_loaded[g % SLOTS[0]], 16)
                    elif kind == "load_sim":
                        g, = args
                        load_sim(sp, g, QS[1], "q", Q_PARTS)
                        if g == NG - 1:
                            sp.wait_ge(pv_done[0], 4 * NG)
                            for e in range(E):
                                sp.dma_start(w1_sb[0:KW, e], w1[e].rearrange("(k p) h -> p k h", k=KC)).then_inc(w1_in, 16)
                            sp.dma_start(w1_sb[KW:KW + 1, :, 0, :], b1.unsqueeze(0)).then_inc(w1_in, 16)
                            sp.wait_ge(zeros_set, 1)
                            sp.dma_start(out[DUMP:DUMP + P, :], zeros[:, :]).then_inc(dump_in, 16)
                    elif kind == "normalise" and args == (NG - 1, 1):
                        wait_filled(sp, unit("normalise", NG - 1, 1))
                        sp.wait_ge(pv_done[0], 4 * NG)
                        for e in range(E):
                            sp.dma_start(w2_sb[:, e], w2[e].rearrange("(k p) d -> p k d", p=P)).then_inc(w2_in, 16)
                    elif kind == "out_norm":
                        b, = args
                        sp.wait_ge(x2_ready, b + 1)
                        rows = slice(b * N, (b + 1) * N)
                        sp.dma_start(x2_rows[rows, :].rearrange("(p c) d -> p c d", c=CT), X2[:, :, :]).then_inc(x2_stored, 16)
                        sp.dma_start(out[rows, :].rearrange("(p c) d -> p c d", c=CT),
                                     H[:, CT * b:CT * (b + 1), :]).then_inc(h_stored, 16)
                sp.wait_ge(lists_ready, 1)
                sp.dma_start(b2_b, b2.partition_broadcast(P)).then_inc(b2_in, 16)
                sp.wait_ge(scattered, 16 * NBLK)

            @block.gpsimd
            def _(pool):
                pool.memset(ident[:, :], 0.0).then_inc(pool_step, 1)
                pool.wait_ge(pool_step, 1)
                pool.affine_select(out=ident[:, :], in_=ident[:, :], compare_op=ALU.not_equal, fill=1.0, base=0,
                                   pattern=[[-1, P]], channel_multiplier=1).then_inc(ident_set, 1)
                pool.wait_ge(rows_ready, 1)
                for t in range(TILES):
                    pool.indirect_dma_start(H[:, t, :], None, table,
                                            bass.IndirectOffsetOnAxis(ap=rows_sb[:, t:t + 1], axis=0)
                                            ).then_inc(gathered[t // CT], 16)
                any_dt = dict(allow_small_or_imprecise_dtypes=True)
                pool.memset(zeros[:, :], 0.0).then_inc(zeros_set, 1)
                pool.memset(ones[:, :], 1.0).then_inc(pool_step, 1)
                pool.memset(not_first[:, :, :], 1.0).then_inc(pool_step, 1)
                pool.iota(slot_no[:, :], pattern=[[1, P]], base=0, channel_multiplier=0, **any_dt)
                pool.iota(block_no[:, :], pattern=[[1, NBLK]], base=0, channel_multiplier=0, **any_dt)
                pool.iota(expert_no[:, :, :], pattern=[[0, TILES], [1, E]], base=0, channel_multiplier=0, **any_dt)
                pool.iota(token_1[:, :].rearrange("p (b c) -> p b c", b=B), pattern=[[N, B], [1, CT]], base=1,
                          channel_multiplier=CT, **any_dt)
                pool.iota(dump_1[:, :], pattern=[[0, 1]], base=DUMP + 1, channel_multiplier=1, **any_dt)
                pool.wait_ge(pool_step, 3)
                pool.affine_select(out=before[:, :], in_=ones[:, :], compare_op=ALU.is_gt, fill=0.0, base=0,
                                   pattern=[[1, P]], channel_multiplier=-1)
                pool.affine_select(out=not_first[:, :, :], in_=not_first[:, :, :], compare_op=ALU.is_gt, fill=0.0, base=0,
                                   pattern=[[0, E], [1, TILES]], channel_multiplier=0).then_inc(iotas_set, 1)
                for kind, args in EVENTS:
                    if kind == "mid":
                        n = SPLIT[(args[0], args[1:])]
                        pool.wait_ge(mid_written, n + 1)
                        part = args[0][0].upper()
                        pool.tensor_tensor(PARTS[part + "L"][:, args[2], :], REST[n % RESTS], PARTS[part + "M"][:, args[2], :],
                                           ALU.subtract).then_inc(lo_written, 1)
                    elif kind == "load_qk":
                        load_qk(pool, args[0], KS[0], "K", K_PARTS)
                    elif kind == "load_sim":
                        load_sim(pool, args[0], KS[1], "k", K_PARTS)

                def gather(j):
                    if j >= 2:
                        pool.wait_ge(xgt_filled, j - 1)
                    pool.indirect_dma_start(XG[j % 2], None, x2_rows,
                                            bass.IndirectOffsetOnAxis(ap=slot_token[:, j:j + 1], axis=0)
                                            ).then_inc(xg_loaded[j % 2], 16)

                pool.wait_ge(lists_ready, 1)
                pool.wait_ge(x2_stored, 16 * B)
                for j in range(3):
                    gather(j)
                pool.wait_ge(h_stored, 16 * B)
                pool.wait_ge(dump_in, 16)
                for j in range(NBLK):
                    if j + 3 < NBLK:
                        gather(j + 3)
                    pool.wait_ge(y_weighted, j + 1)
                    if j >= 1:
                        pool.wait_ge(scattered, 16 * j)
                    pool.indirect_dma_start(out, bass.IndirectOffsetOnAxis(ap=slot_dest[:, j:j + 1], axis=0), Y[j % 2], None,
                                            compute_op=ALU.add).then_inc(scattered, 16)

            @block.scalar
            def _(act):
                for kind, args in EVENTS:
                    if kind not in PSUM_KINDS and kind not in ("pv", "mid"):
                        continue
                    if kind == "mid":
                        n = SPLIT[(args[0], args[1:])]
                        wait_consumed(act, unit(*args))
                        act.activation(PARTS[args[0][0].upper() + "M"][:, args[2], :], REST[n % RESTS], ACT.Copy).then_inc(mid_written, 1)
                        continue
                    if kind == "pv":
                        g, u, j, ps = args
                        if (u, j) == (1, 1):
                            act.wait_ge(pv_done[ps], 4 * g + 4)
                            if g >= 1:
                                wait_filled(act, unit("normalise", g - 1, ps))
                            act.activation(ACCS[:, ps, :], acc[ps], ACT.Copy).then_inc(acc_saved[ps], 1)
                        continue
                    k = unit(kind, *args)
                    done = freed[k % RING]
                    s = slot(k)
                    if kind == "x_transpose":
                        b, j = args
                        wait_filled(act, k)
                        if b >= 1:
                            wait_filled(act, unit("v_proj", b - 1, 1))
                        act.activation(XT[0:KW, j, :], s[0:KW], ACT.Copy).then_inc(done, 1)
                    elif kind in ("q_proj", "k_proj", "t_transpose"):
                        b, j = args
                        wait_filled(act, k)
                        if b >= 1:
                            loaded = {"q_proj": [qk_loaded["q"]], "k_proj": [qk_loaded["k"]],
                                      "t_transpose": [sim_loaded["q"], sim_loaded["k"]]}[kind]
                            for side in loaded:
                                for g in range(max(0, GB * b - len(side)), GB * b):
                                    act.wait_ge(side[g % len(side)], LOADS * (g // len(side) + 1))
                        act.activation(PARTS[kind[0].upper() + "H"][:, j, :], s, ACT.Copy).then_inc(hi_written, 1)
                    elif kind == "v_proj":
                        b, j = args
                        wait_filled(act, k)
                        act.activation(V[b][:, 2 * j:2 * j + 2, :, 0:D],
                                       slot_tiles(k).rearrange("p c (h d) -> p c h d", d=D), ACT.Copy).then_inc(done, 1)
                    elif kind == "max_row":
                        g, = args
                        wait_filled(act, k)
                        if g >= 2:
                            act.wait_ge(row_loaded[(g - 2) % SLOTS[0]], 32 * ((g - 2) // SLOTS[0] + 1))
                        act.activation(MRH[:, g % 2, :], s[0:4 * GH, 0:P], ACT.Copy, scale=-1.0).then_inc(row_hi, 1)
                    elif kind in ("exp_unit", "sim_unit"):
                        g, q, j = args
                        c = UG * g + q
                        ps = int(kind == "sim_unit")
                        wait_filled(act, k)
                        if c >= PRING:
                            act.wait_ge(pv_done[ps], 2 * ((c - PRING) // GH) + 2)
                        act.activation((P1, P2)[ps][:, c % PRING, j, :], s, ACT.Exp,
                                       scale=(QSCALE, SIM_SCALE)[ps]).then_inc(done, 1)
                    elif kind in ("o_transpose", "gate_transpose"):
                        wait_filled(act, k)
                        for reader, j in (("proj_norm", 1), ("proj_out", 1)):
                            before_k = [unit(reader, n, j) for n in range(B) if unit(reader, n, j) < k]
                            if before_k:
                                wait_filled(act, max(before_k))
                        before_k = [unit("gate_logits", n) for n in range(B) if unit("gate_logits", n) < k]
                        if before_k:
                            wait_filled(act, max(before_k))
                        act.activation(OT[0:KW, args[-1], :], s[0:KW], ACT.Copy).then_inc(done, 1)
                    elif kind == "proj_norm":
                        wait_filled(act, k)
                        b, j = args
                        if b >= 1:
                            wait_filled(act, unit("t_transpose", b - 1, 1))
                        if b >= 1:
                            act.wait_ge(t_ready, b)
                        act.activation(SQ[:, 2 * j:2 * j + 2, :], slot_tiles(k), ACT.Square).then_inc(sq_done, 1)
                        act.activation(T[:, 2 * j:2 * j + 2, :], slot_tiles(k), ACT.Copy).then_inc(done, 1)

                act.wait_ge(shifted, 1)
                act.activation(rt["b"][:, :, :], rt["a"][:, :, :], ACT.Exp).then_inc(exped, 1)

                def step(j, i):
                    act.wait_ge(hid_filled, j + 1)
                    wait_past(act, y_filled, j - 1)
                    act.activation(HT[i].rearrange("p k t -> p (k t)"), hid_ps[i], ACT.Gelu).then_inc(hid_done, 1)

                over_blocks(act, step)

            @block.vector
            def _(dve):
                steps = [0]

                def link(ins):
                    steps[0] += 1
                    ins.then_inc(dve_step, 1)
                    dve.wait_ge(dve_step, steps[0])

                def rsqrt(dst, src, floor, add, n):
                    x, y, t = (nt[i][:, 0:n] for i in range(3))
                    link(dve.tensor_scalar(x, src, floor, add, ALU.max, ALU.add))
                    link(dve.tensor_scalar(t.bitcast(I32), x.bitcast(I32), 1, None, ALU.arith_shift_right))
                    link(dve.tensor_scalar(y.bitcast(I32), t.bitcast(I32), -1.0, float(RSQRT_MAGIC), ALU.mult, ALU.add))
                    for i in range(3):
                        link(dve.tensor_tensor(t, y, y, ALU.mult))
                        link(dve.scalar_tensor_tensor(t, t, -0.5, x, ALU.mult, ALU.mult))
                        link(dve.scalar_tensor_tensor(dst if i == 2 else y, t, 1.5, y, ALU.add, ALU.mult))

                def norm_stats(mean_var, rstd, src, eps):
                    n = src.shape[1]
                    for c in range(n):
                        last = dve.bn_stats(stats[:, c, :], src[:, c, :])
                    link(last)
                    for c in range(n):
                        last = dve.bn_aggr(mean_var[:, c, :], stats[:, c, :])
                    link(last)
                    rsqrt(rstd, mean_var[:, :, 1], 0.0, eps, n)

                def norm_apply(dst, src, mean_var, rstd):
                    for c in range(src.shape[1]):
                        last = dve.tensor_scalar(dst[:, c, :], src[:, c, :], mean_var[:, c, 0:1], rstd[:, c:c + 1],
                                                 ALU.subtract, ALU.mult)
                    return last

                def layer_norm(dst, src, eps):
                    n = src.shape[1]
                    norm_stats(mv[:, 0:n, :], nt[3][:, 0:n], src, eps)
                    return norm_apply(dst, src, mv, nt[3])

                dve.wait_ge(ids_in, 16)
                dve.tensor_scalar(rows_sb[:, :], ids_sb[:, :], BUCKETS - 1, None, ALU.bitwise_and).then_inc(rows_ready, 1)
                dve.memset(XT[KW:KW + 1, 0, :], 1.0)
                dve.memset(OT[KW:KW + 1, 0, :], 1.0).then_inc(consts_set, 1)

                for kind, args in EVENTS:
                    k = unit(kind, *args) if kind in PSUM_KINDS else None
                    if kind == "embed_norm":
                        b0, b1 = args
                        h = H[:, CT * b0:CT * b1, :]
                        for b in range(b0, b1):
                            dve.wait_ge(gathered[b], 16 * CT)
                        link(layer_norm(h, h, 1e-6))
                        dve.wait_ge(lnw_in, 32)
                        n = h.shape[1]
                        link(dve.tensor_tensor(h, h, scale_b[:, :].unsqueeze(1).to_broadcast([P, n, C]), ALU.mult))
                        link(dve.tensor_tensor(h, h, bias_b[:, :].unsqueeze(1).to_broadcast([P, n, C]), ALU.add))
                    elif kind == "attn_stats":
                        b0, b1 = args
                        tiles = slice(CT * b0, CT * b1)
                        norm_stats(mv_x[:, tiles, :], rstd_x[:, tiles], H[:, tiles, :], 1e-5)
                    elif kind == "attn_norm":
                        b, = args
                        tiles = slice(CT * b, CT * (b + 1))
                        if b == 0:
                            norm_stats(mv_x[:, tiles, :], rstd_x[:, tiles], H[:, tiles, :], 1e-5)
                        else:
                            wait_filled(dve, unit("x_transpose", b - 1, 1))
                        norm_apply(X, H[:, tiles, :], mv_x[:, tiles, :], rstd_x[:, tiles]).then_inc(x_ready, 1)
                        if b == 0:
                            for n in range(SLOTS[0]):
                                dve.memset(KS[0][n][SD:SD + 2, :, :], 1.0)
                            dve.memset(acc[0], 0.0)
                            dve.memset(acc[1], 0.0)
                            for n in range(B):
                                last = dve.memset(V[n][:, :, :, D:VW], 1.0)
                            last.then_inc(ones_set, 1)
                    elif kind in ("q_proj", "k_proj", "t_transpose"):
                        n = SPLIT[(kind, args)]
                        dve.wait_ge(hi_written, n + 1)
                        if n >= RESTS:
                            dve.wait_ge(lo_written, n - RESTS + 1)
                        dve.tensor_tensor(REST[n % RESTS], slot(k), PARTS[kind[0].upper() + "H"][:, args[1], :], ALU.subtract).then_inc(freed[k % RING], 1)
                    elif kind == "max_unit":
                        g, q, j = args
                        i, u = q % GH, q // GH
                        if q == 0 and j == 0 and g >= 2:
                            wait_filled(dve, unit("max_row", g - 2))
                        wait_filled(dve, k)
                        dve.tensor_reduce(MX[:, g % 2, 4 * i + 2 * u + j:4 * i + 2 * u + j + 1], slot(k), AX_X, ALU.max
                                          ).then_inc(freed[k % RING], 1)
                    elif kind == "max_row":
                        g, = args
                        dve.wait_ge(row_hi, g + 1)
                        dve.scalar_tensor_tensor(MRM[:, g % 2, :], slot(k)[0:4 * GH, 0:P], -1.0,
                                                 MRH[:, g % 2, :], ALU.mult, ALU.subtract
                                                 ).then_inc(freed[k % RING], 1)
                    elif kind == "mask":
                        g, q = args
                        wait_consumed(dve, unit("sim_unit", g, q, 0))
                        wait_consumed(dve, unit("sim_unit", g, q, 1))
                        p = P2[:, (UG * g + q) % PRING, :, :]
                        dve.scalar_tensor_tensor(p, p, 1.0, p, ALU.is_ge, ALU.mult).then_inc(masked, 1)
                    elif kind == "normalise":
                        g, ps = args
                        wait_filled(dve, k)
                        v = slot(k).rearrange("p (c h w) -> p c h w", c=CT, h=GH)
                        link(dve.reciprocal(rec[:, :, :], v[:, :, :, D]))
                        if g % GB == 0:
                            if g >= GB:
                                wait_filled(dve, unit("o_transpose", g // GB - 1, ps, 1))
                        o = O[ps][:, :, (g % GB) * GH * D:(g % GB + 1) * GH * D].rearrange("p c (h d) -> p c h d", d=D)
                        dve.tensor_tensor(o, v[:, :, :, 0:D], rec[:, :, :].unsqueeze(3).to_broadcast([P, CT, GH, D]),
                                          ALU.mult).then_inc(freed[k % RING], 1)
                    elif kind == "unit_tokens":
                        b, = args
                        dve.wait_ge(sq_done, 2 * (b + 1))
                        ss = nt[3][:, 0:CT * NH]
                        squares = SQ[:, :, :].rearrange("p c (g d h) -> p (c g) d h", g=GB, h=GH)
                        link(dve.tensor_reduce(ss, squares.rearrange("p x d h -> p x h d"), AX_X, ALU.add))
                        rsqrt(ss, ss, 1e-24, 0.0, CT * NH)
                        wait_consumed(dve, unit("proj_norm", b, 0))
                        wait_consumed(dve, unit("proj_norm", b, 1))
                        tiles = T[:, :, :].rearrange("p c (g d h) -> p (c g) d h", g=GB, h=GH)
                        dve.tensor_tensor(tiles, tiles, ss.rearrange("p (x h) -> p x h", h=GH).unsqueeze(2).to_broadcast(
                            [P, CT * GB, D, GH]), ALU.mult).then_inc(t_ready, 1)
                    elif kind == "proj_out":
                        b, j = args
                        h = H[:, CT * b + 2 * j:CT * b + 2 * j + 2, :]
                        wait_filled(dve, k)
                        dve.tensor_tensor(h, slot_tiles(k), h, ALU.add).then_inc(freed[k % RING], 1)
                    elif kind == "out_norm":
                        b, = args
                        for j in range(2):
                            wait_consumed(dve, unit("proj_out", b, j))
                        if b >= 1:
                            dve.wait_ge(x2_stored, 16 * b)
                            wait_filled(dve, unit("gate_transpose", b - 1, 1))
                        layer_norm(X2, H[:, CT * b:CT * (b + 1), :], 1e-5).then_inc(x2_ready, 1)
                    elif kind == "gate_logits":
                        b, = args
                        wait_filled(dve, k)
                        dve.tensor_copy(LG[:, CT * b:CT * (b + 1), :],
                                        slot(k)[:, 0:CT * E].rearrange("p (c e) -> p c e", e=E)).then_inc(freed[k % RING], 1)

                def per_expert(v):
                    return v.unsqueeze(2).to_broadcast([P, TILES, E])

                a, bb, prob = rt["a"][:, :, :], rt["b"][:, :, :], rt["prob"][:, :, :]
                m, r = col["m"][:, :], col["r"][:, :]
                wait_consumed(dve, unit("gate_logits", B - 1))
                dve.wait_ge(iotas_set, 1)
                link(dve.tensor_reduce(m, LG[:, :, :], AX_X, ALU.max))
                dve.tensor_tensor(a, LG[:, :, :], per_expert(m), ALU.subtract).then_inc(shifted, 1)
                dve.wait_ge(exped, 1)
                link(dve.tensor_reduce(m, bb, AX_X, ALU.add))
                link(dve.reciprocal(r, m))
                link(dve.tensor_tensor(prob, bb, per_expert(r), ALU.mult))
                for n in range(TOPK):
                    top, oh = col[f"p{n}"][:, :], rt[f"oh{n}"][:, :, :]
                    link(dve.tensor_reduce(top, prob, AX_X, ALU.max))
                    link(dve.tensor_tensor(a, prob, per_expert(top), ALU.is_equal))
                    link(dve.scalar_tensor_tensor(a, a, -float(E), expert_no[:, :, :], ALU.mult, ALU.add))
                    link(dve.tensor_reduce(m, a, AX_X, ALU.min))
                    link(dve.tensor_tensor(oh, a, per_expert(m), ALU.is_equal))
                    if n == 0:
                        link(dve.scalar_tensor_tensor(prob, oh, -4.0, prob, ALU.mult, ALU.add))
                oh0, oh1 = rt["oh0"][:, :, :], rt["oh1"][:, :, :]
                dve.tensor_tensor(bb, oh0, oh1, ALU.add).then_inc(chosen, 1)
                link(dve.scalar_tensor_tensor(m, col["p0"][:, :], 1e-9, col["p1"][:, :], ALU.add, ALU.add))
                link(dve.reciprocal(r, m))
                for n in range(TOPK):
                    dve.tensor_tensor(weight[:, n, :], col[f"p{n}"][:, :], r, ALU.mult)
                dve.wait_ge(counted, 1)
                tot, inc = a.rearrange("p t e -> p (t e)").rearrange("p (e t) -> p e t", e=E), prob.rearrange("p t e -> p (t e)").rearrange("p (e t) -> p e t", e=E)
                link(dve.tensor_copy(tot, psum[:, 1, 0:P].rearrange("p (t e) -> p e t", e=E)))
                link(dve.tensor_tensor_scan(prob.rearrange("p t e -> p (t e)"), not_first[:, :, :].rearrange("p e t -> p (e t)"),
                                            a.rearrange("p t e -> p (t e)"), 0.0, ALU.mult, ALU.add))
                cnt, end, base = (exp8[nm][:, :] for nm in ("n", "end", "base"))
                link(dve.tensor_scalar(exp8_i[:, :], inc[:, :, TILES - 1], float(P - 1), None, ALU.add))
                link(dve.tensor_scalar(exp8_i[:, :], exp8_i[:, :], P.bit_length() - 1, None, ALU.arith_shift_right))
                link(dve.tensor_copy(cnt, exp8_i[:, :]))
                link(dve.tensor_tensor_scan(end, ones[:, 0:E], cnt, 0.0, ALU.mult, ALU.add))
                link(dve.tensor_tensor(base, end, cnt, ALU.subtract))
                link(dve.tensor_tensor(inc, inc, tot, ALU.subtract))
                link(dve.scalar_tensor_tensor(inc, base.unsqueeze(2).to_broadcast([P, E, TILES]), float(P), inc, ALU.mult, ALU.add))
                link(dve.tensor_tensor(bb, psum[:, 0, 0:P].rearrange("p (t e) -> p t e", e=E), inc.rearrange("p e t -> p t e"), ALU.add))
                for n in range(TOPK):
                    link(dve.tensor_tensor(a, bb, rt[f"oh{n}"][:, :, :], ALU.mult))
                    link(dve.tensor_reduce(place[:, n, :], a, AX_X, ALU.add))
                link(dve.tensor_copy(place_i[:, :, :], place[:, :, :]))
                link(dve.tensor_scalar(part_i[:, :, :], place_i[:, :, :], P - 1, None, ALU.bitwise_and))
                link(dve.tensor_copy(row_f[:, :, :], part_i[:, :, :]))
                link(dve.tensor_scalar(part_i[:, :, :], place_i[:, :, :], P.bit_length() - 1, None, ALU.arith_shift_right))
                link(dve.tensor_copy(blk_f[:, :, :], part_i[:, :, :]))
                blk = blk_f[:, :, :].rearrange("p n t -> p (n t)")
                link(dve.tensor_tensor(oh_blk, block_no[:, :].unsqueeze(1).to_broadcast([P, NQ, NBLK]),
                                       blk.unsqueeze(2).to_broadcast([P, NQ, NBLK]), ALU.is_equal))
                for n in range(TOPK):
                    dve.tensor_tensor(tag[:, n * TILES:(n + 1) * TILES, 0, :], oh_blk[:, n * TILES:(n + 1) * TILES, :],
                                      token_1[:, :].unsqueeze(2).to_broadcast([P, TILES, NBLK]), ALU.mult)
                dve.tensor_tensor(tag[:, :, 1, :], oh_blk, weight[:, :, :].rearrange("p n t -> p (n t)").unsqueeze(2).to_broadcast([P, NQ, NBLK]),
                                  ALU.mult).then_inc(tags_ready, 1)
                rows = row_f[:, :, :].rearrange("p n t -> p (n t)")
                for q in range(NQ):
                    if q >= OHR:
                        dve.wait_ge(row_used, q - OHR + 1)
                    dve.tensor_scalar(oh_row[:, q % OHR, :], slot_no[:, :], rows[:, q:q + 1], None, ALU.is_equal).then_inc(row_ready, 1)
                link(dve.tensor_tensor(blk_ge, block_no[0:1, :].unsqueeze(2).to_broadcast([1, NBLK, E]),
                                       end[0:1, :].unsqueeze(1).to_broadcast([1, NBLK, E]), ALU.is_ge))
                link(dve.tensor_reduce(blk_expert_f[:, :], blk_ge, AX_X, ALU.add))
                dve.tensor_scalar(blk_expert[:, :], blk_expert_f[:, :], float(E - 1), None, ALU.min)
                dve.wait_ge(listed, 1)
                tok = psum[:, 2, 0:NBLK]
                dve.tensor_copy(slot_weight[:, :], psum[:, 2, NBLK:2 * NBLK])
                dve.tensor_scalar(slot_token[:, :], tok, -1.0, 0.0, ALU.add, ALU.max)
                link(dve.tensor_scalar(slot_tmp[:, :], tok, 0.0, dump_1[:, 0:1], ALU.is_equal, ALU.mult))
                dve.scalar_tensor_tensor(slot_dest[:, :], tok, -1.0, slot_tmp[:, :], ALU.add, ALU.add).then_inc(lists_ready, 1)
                dve.wait_ge(lists_ready, 1)

                def stage(j, i):
                    e = dve.value_load(blk_expert[0:1, bass.ds(j, 1)], min_val=0, max_val=E - 1)
                    wait_past(dve, hid_filled, j - 1)
                    dve.tensor_copy(W1S[i][0:KW, 1, :], w1_sb[0:KW, bass.ds(e, 1), 1, :].rearrange("p o h -> p (o h)"))
                    dve.tensor_copy(W1S[i][0:KW + 1, 0, :], w1_sb[0:KW + 1, bass.ds(e, 1), 0, :].rearrange("p o h -> p (o h)")).then_inc(w1_staged, 1)

                def take_tokens(j, i):
                    dve.wait_ge(xgt_filled, j + 1)
                    dve.tensor_copy(XGT[i][0:KW, :, :], xgt_ps[i]).then_inc(xgt_ready, 1)

                def step(j, i):
                    if not isinstance(j, int) or j + 2 < NBLK:
                        stage(j + 2, i)
                        take_tokens(j + 2, i)
                    e = dve.value_load(blk_expert[0:1, bass.ds(j, 1)], min_val=0, max_val=E - 1)
                    dve.wait_ge(y_filled, j + 1)
                    wait_past(dve, scattered, 16 * (j - 1))
                    dve.tensor_tensor(Y[i], y_ps[i], b2_b[:, bass.ds(e, 1), :].rearrange("p o d -> p (o d)"), ALU.add).then_inc(y_biased, 1)
                    dve.wait_ge(y_biased, j + 1)
                    dve.tensor_scalar(Y[i], Y[i], slot_weight[:, bass.ds(j, 1)], None, ALU.mult).then_inc(y_weighted, 1)

                dve.wait_ge(w1_in, 16 * (E + 1))
                for j in range(2):
                    stage(j, j)
                    take_tokens(j, j)
                dve.wait_ge(b2_in, 16)
                over_blocks(dve, step)

            @block.tensor
            def _(pe):
                pe.wait_ge(ident_set, 1)
                for kind, args in EVENTS:
                    if kind == "pv":
                        if args == (0, 0, 0, 0):
                            pe.wait_ge(ones_set, 1)
                        g, u, j, ps = args
                        b = g // GB
                        if ps == 0:
                            for q in range(GH * u, GH * u + GH):
                                wait_consumed(pe, unit("exp_unit", g, q, j))
                            wait_consumed(pe, unit("v_proj", b, u))
                        else:
                            pe.wait_ge(masked, UG * g + GH * (u + 1))
                        if u == 0 and j == 0 and g >= 1:
                            pe.wait_ge(acc_saved[ps], g)
                        for i in range(GH):
                            c = UG * g + GH * u + i
                            last = pe.matmul(acc[ps][32 * i:32 * i + VW, :], V[b][:, 2 * u + j, GH * (g % GB) + i, :],
                                             (P1, P2)[ps][:, c % PRING, j, :], start=(u == 0 and j == 0),
                                             stop=(u == 1 and j == 1))
                        last.then_inc(pv_done[ps], 1)
                        continue
                    if kind not in PSUM_KINDS:
                        continue
                    k = unit(kind, *args)
                    s = slot(k)
                    if k >= RING:
                        wait_consumed(pe, k - RING)
                    if kind in ("x_transpose", "t_transpose", "o_transpose", "gate_transpose"):
                        b, kc = args[0], args[-1]
                        src = O[args[1]] if kind == "o_transpose" else {"x_transpose": X, "t_transpose": T, "gate_transpose": X2}[kind]
                        if kind == "x_transpose":
                            pe.wait_ge(x_ready, b + 1)
                        elif kind == "gate_transpose":
                            pe.wait_ge(x2_ready, b + 1)
                        elif kind == "t_transpose":
                            pe.wait_ge(t_ready, b + 1)
                        else:
                            for g in range(GB * b, GB * b + GB):
                                wait_consumed(pe, unit("normalise", g, args[1]))
                        width, stride = (2 * GC, GC) if kind == "t_transpose" else (KW, KW)
                        for c in range(CT):
                            last = pe.transpose(s[0:width, c * P:(c + 1) * P], src[:, c, kc * stride:kc * stride + width],
                                                ident[:, :])
                    elif kind in ("q_proj", "k_proj"):
                        b, m = args
                        m0 = C * (kind == "k_proj") + m * GC
                        for kc in range(KC):
                            wait_consumed(pe, unit("x_transpose", b, kc))
                        if b == 0:
                            pe.wait_ge(wqkv_in, 32)
                            pe.wait_ge(consts_set, 1)
                        for kc in range(KC):
                            rows = KW + (kc == 0)
                            last = pe.matmul(s, WQKV[0:rows, kc, m0:m0 + 2 * GC], XT[0:rows, kc, :], start=kc == 0, stop=kc == KC - 1)
                    elif kind == "v_proj":
                        b, j = args
                        for kc in range(KC):
                            wait_consumed(pe, unit("x_transpose", b, kc))
                        for c in range(2):
                            for kc in range(KC):
                                rows = KW + (kc == 0)
                                last = pe.matmul(slot_tiles(k)[:, c, :], XT[0:rows, kc, (2 * j + c) * P:(2 * j + c + 1) * P],
                                                 WQKV[0:rows, kc, 2 * C:3 * C], start=kc == 0, stop=kc == KC - 1)
                    elif kind == "max_unit":
                        g, q, j = args
                        i, c, sl = q % GH, 2 * (q // GH) + j, g % SLOTS[0]
                        if (q, j) == (0, 0):
                            for side in "qk":
                                pe.wait_ge(qk_loaded[side][sl], LOADS * (g // SLOTS[0] + 1))
                        last = pe.matmul(s, QS[0][sl][0:SD, i, c * P:(c + 1) * P], KS[0][sl][0:SD, i, :], start=True, stop=True)
                    elif kind == "exp_unit":
                        g, q, j = args
                        i, c, sl = q % GH, 2 * (q // GH) + j, g % SLOTS[0]
                        if (g, q, j) == (0, 0, 0):
                            pe.wait_ge(ones_set, 1)
                        if (q, j) == (0, 0):
                            pe.wait_ge(row_loaded[sl], 32 * (g // SLOTS[0] + 1))
                        last = pe.matmul(s, KS[0][sl][:, i, c * P:(c + 1) * P], QS[0][sl][:, i, :], start=True, stop=True)
                    elif kind == "sim_unit":
                        g, q, j = args
                        i, c, sl = q % GH, 2 * (q // GH) + j, g % SLOTS[1]
                        if (q, j) == (0, 0):
                            for side in "qk":
                                pe.wait_ge(sim_loaded[side][sl], LOADS * (g // SLOTS[1] + 1))
                        last = pe.matmul(s, QS[1][sl][:, i, c * P:(c + 1) * P], KS[1][sl][:, i, :], start=True, stop=True)
                    elif kind == "max_row":
                        g, = args
                        for q in range(UG - 2, UG):
                            for j in range(2):
                                wait_consumed(pe, unit("max_unit", g, q, j))
                        last = pe.transpose(s[0:4 * GH, 0:P], MX[:, g % 2, :], ident[:, :])
                    elif kind == "normalise":
                        g, ps = args
                        pe.wait_ge(acc_saved[ps], g + 1)
                        for c in range(CT):
                            last = pe.transpose(s[:, c * P:(c + 1) * P], ACCS[:, ps, c * P:(c + 1) * P], ident[:, :])
                    elif kind in ("proj_norm", "proj_out"):
                        b, j = args
                        norm = kind == "proj_norm"
                        for kc in range(KC):
                            wait_consumed(pe, unit("o_transpose", b, int(not norm), kc))
                        if b == 0:
                            pe.wait_ge(pw_in, 64)
                        for c in range(2):
                            for kc in range(KC):
                                rows = KW + (kc == 0)
                                last = pe.matmul(slot_tiles(k)[:, c, :], OT[0:rows, kc, (2 * j + c) * P:(2 * j + c + 1) * P],
                                                 (PWN if norm else PW)[0:rows, kc, :], start=kc == 0, stop=kc == KC - 1)
                    elif kind == "gate_logits":
                        b, = args
                        for kc in range(KC):
                            wait_consumed(pe, unit("gate_transpose", b, kc))
                        if b == 0:
                            pe.wait_ge(gt_in, 16)
                        for c in range(CT):
                            for kc in range(KC):
                                last = pe.matmul(s[:, c * E:(c + 1) * E], OT[0:KW, kc, c * P:(c + 1) * P], GT[:, kc, :],
                                                 start=kc == 0, stop=kc == KC - 1)
                    last.then_inc(filled[k % RING], 1)

                chose = rt["b"][:, :, :].rearrange("p t e -> p (t e)")
                pe.wait_ge(chosen, 1)
                pe.wait_ge(iotas_set, 1)
                pe.matmul(psum[:, 0, 0:P], before[:, :], chose, start=True, stop=True)
                pe.matmul(psum[:, 1, 0:P], ones[:, :], chose, start=True, stop=True).then_inc(counted, 1)
                pe.wait_ge(tags_ready, 1)
                for q in range(NQ):
                    pe.wait_ge(row_ready, q + 1)
                    last = pe.matmul(psum[:, 2, 0:2 * NBLK], oh_row[:, q % OHR, :], tag[:, q, :, :].rearrange("p s j -> p (s j)"),
                                     start=q == 0, stop=q == NQ - 1)
                    last.then_inc(row_used if q < NQ - 1 else listed, 1)

                def turn(j, i):
                    pe.wait_ge(xg_loaded[i], 8 * (j + 2 - i))
                    wait_past(pe, xgt_ready, j - 1)
                    for kc in range(KC):
                        last = pe.transpose(xgt_ps[i][:, kc, :], XG[i][:, kc * KW:(kc + 1) * KW], ident[:, :])
                    last.then_inc(xgt_filled, 1)

                def first_layer(j, i):
                    pe.wait_ge(xgt_ready, j + 1)
                    pe.wait_ge(w1_staged, j + 1)
                    wait_past(pe, hid_done, j - 1)
                    for hc in range(HC):
                        for kc in range(KC):
                            rows = KW + (kc == 0)
                            last = pe.matmul(hid_ps[i][:, hc * P:(hc + 1) * P], W1S[i][0:rows, kc, hc * P:(hc + 1) * P],
                                             XGT[i][0:rows, kc, :], start=kc == 0, stop=kc == KC - 1)
                    last.then_inc(hid_filled, 1)

                def second_layer(j, i):
                    e = pe.value_load(blk_expert[0:1, bass.ds(j, 1)], min_val=0, max_val=E - 1)
                    pe.wait_ge(hid_done, j + 1)
                    wait_past(pe, y_weighted, j - 1)
                    for hc in range(HC):
                        last = pe.matmul(y_ps[i], HT[i][:, hc, :], w2_sb[:, bass.ds(e, 1), hc, :].rearrange("p o d -> p (o d)"),
                                         start=hc == 0, stop=hc == HC - 1)
                    last.then_inc(y_filled, 1)

                def step(j, i):
                    if not isinstance(j, int) or j + 2 < NBLK:
                        turn(j + 2, i)
                    if not isinstance(j, int) or j + 1 < NBLK:
                        first_layer(j + 1, (i + 1) % 2)
                    second_layer(j, i)

                pe.wait_ge(lists_ready, 1)
                turn(0, 0)
                turn(1, 1)
                first_layer(0, 0)
                pe.wait_ge(w2_in, 16 * E)
                over_blocks(pe, step)


def kernel(x, L0_tok_tables, L0_tok_ln_scale, L0_tok_ln_bias, L0_attn_qkv_w, L0_attn_qkv_b, L0_attn_proj_w,
           L0_attn_proj_b, L0_ffn_gate_w, L0_ffn_w1, L0_ffn_b1, L0_ffn_w2, L0_ffn_b2):
    import numpy as np
    import concourse.bacc as bacc
    from concourse.bass_utils import run_bass_kernel_spmd

    primes = (31, 43, 59, 61, 73, 97, 103, 113)
    r = np.arange(BUCKETS)
    tables = np.asarray(L0_tok_tables)
    table = np.concatenate([tables[h][(r + 1) * p % BUCKETS] for h, p in enumerate(primes)], axis=1)
    by_width = np.arange(C).reshape(GB, GH, D).transpose(0, 2, 1).reshape(-1)
    qkv_cols = np.concatenate([by_width, C + by_width, 2 * C + np.arange(C)])
    proj_wt = np.asarray(L0_attn_proj_w).T
    arrays = {
        "ids": np.asarray(x), "table": table, "ln_scale": L0_tok_ln_scale, "ln_bias": L0_tok_ln_bias,
        "qkv_wt": np.asarray(L0_attn_qkv_w).T[:, qkv_cols], "qkv_b": np.asarray(L0_attn_qkv_b)[qkv_cols],
        "proj_wt": proj_wt, "proj_b": L0_attn_proj_b,
        "proj_wt_n": proj_wt[:, by_width], "proj_b_n": np.asarray(L0_attn_proj_b)[by_width],
        "gate_wt": np.asarray(L0_ffn_gate_w).T, "w1": L0_ffn_w1, "b1": L0_ffn_b1, "w2": L0_ffn_w2, "b2": L0_ffn_b2,
    }
    arrays = {k: np.ascontiguousarray(v) for k, v in arrays.items()}
    nc = bacc.Bacc("TRN2", target_bir_lowering=False, num_devices=1)
    args = [nc.dram_tensor(k, a.shape, mybir.dt.from_np(a.dtype), kind="ExternalInput").ap() for k, a in arrays.items()]
    result = nc.dram_tensor("result", (B * N + P, C), F32, kind="ExternalOutput").ap()
    build(nc, *args, result)
    r = run_bass_kernel_spmd(nc, [arrays], core_ids=[0])
    return r.results[0]["result"][:B * N].reshape(B, N, C)
```

```python
from contextlib import ExitStack

import concourse.bass as bass
from concourse import mybir

F32 = mybir.dt.float32
BF16 = mybir.dt.bfloat16
I32 = mybir.dt.int32
U32 = mybir.dt.uint32
ALU = mybir.AluOpType
ACT = mybir.ActivationFunctionType
AX_X = mybir.AxisListType.X

P = 128
B, N, C = 4, 512, 192
NH, D = 12, 16
BUCKETS = 4096
CT = N // P
TILES = B * CT
KC, KW = 2, 96
GH = 4
GB = NH // GH
NG = B * GB
GC = GH * D
Q_PARTS, K_PARTS = "HMHMHL", "HHMMLH"
Q_ORDER, K_ORDER = (0, 2, 4, 1, 3, 5), (0, 1, 5, 2, 3, 4)
SD = len(Q_PARTS) * D
SLOTS = (4, 2)
UG = 2 * GH
VW = D + 1
E, HID = 8, 768
HC = HID // P
TOPK = 2
NBLK = (B * N * TOPK) // P + E - 1
DUMP = B * N
QSCALE = D ** -0.5
SIM_SCALE = 10.0
RING = 6
PRING = 12
RSQRT_MAGIC = 0x5F3759DF

OFF_C, OFF_E = 11, 54
RSQRT_OPS = 12
NORM = ("stats", "moments", *range(RSQRT_OPS))
IN_NORMS = [("embed_norm", x) for x in (*NORM, "apply", "scale", "bias")] + [("attn_stats", x) for x in NORM]


def schedule():
    ev = []

    def at(t, rank, kind, *args):
        ev.append((t, rank, kind, args))

    for b in range(B):
        a = GB * UG * b
        first, last = b == 0, b == B - 1
        for i, (norm, part) in enumerate(IN_NORMS):
            at({0: -9, 1: -3 + i / 10}.get(b, a - 40 + i / 3), 1, norm, b, part)
        at(-8 if first else a - 21, 0, "attn_norm", b)
        for j in range(2):
            h = j / 2
            at(-7 + h if first else a - 16.5 + h, 0, "x_transpose", b, j)
            at(-6 + h if first else a - 15 + j, 0, "q_proj", b, j)
            at(-5 + h if first else a - 13.5 + j, 0, "k_proj", b, j)
            at(-5 + h if first else a - 14 + j, 1, "mid", "q_proj", b, j)
            at(-4 + h if first else a - 11 + j, 0, "v_proj", b, j)
            at(-4 + h if first else a - 12 + j, 1, "mid", "k_proj", b, j)
        d = a + GB * UG - UG + OFF_C + UG + 4.25
        f = a + GB * UG - UG + OFF_E + UG + 5
        for j in range(2):
            h = j / 2
            at(d + h, 6, "o_transpose", b, 0, j)
            at(d + 1.5 + 2 * h, 6, "proj_norm", b, j)
            at(d + (3.5 if last else 8) + h, 6, "t_transpose", b, j)
            at(d + (4 if last else 8.75) + h, 6, "mid", "t_transpose", b, j)
            at(f + h, 6, "o_transpose", b, 1, j)
            at(f + 2.25 + h, 6, "proj_out", b, j)
            at(f + 9 + h, 6, "gate_transpose", b, j)
        at(d + 2.6 if last else d + 2.8, 6, "unit_tokens", b, "squares")
        at(f + 3, 6, "out_norm", b, "stats")
        at(f + 3.5, 6, "out_norm", b, "moments")
        for i in range(RSQRT_OPS):
            at(d + 2.7 if last else d + 3.2 + i / 3, 6, "unit_tokens", b, i)
            at(f + 4 + i / 3, 6, "out_norm", b, i)
        at(d + 2.8 if last else d + 7.5, 6, "unit_tokens", b, "scale")
        at(f + 7.8, 6, "out_norm", b, "apply")
        at(f + 12, 6, "gate_logits", b)
    for g in range(NG):
        a = UG * g
        b = g // GB
        ready = GB * UG * b + GB * UG - UG + OFF_C + UG + 4.5 + (4.6 if b == B - 1 else 8.4)
        for r in range(len(Q_PARTS)):
            if g == 0:
                at(-4.7 if r < 3 else -3.2, 1, "load_qk", g, r)
            else:
                at(-3 + g if g < GB else a - (12.5 if g % GB else 8) + r / 2, 1, "load_qk", g, r)
            at(max(ready, a + OFF_E - 8) + r / 2, 7, "load_sim", g, r)
        for q in range(UG):
            for j in range(2):
                at(a + q + j / 2, 2, "max_unit", g, q, j)
                at(a + OFF_C + q + j / 2 - 0.25, 3, "exp_unit", g, q, j)
                at(a + OFF_E + q + j / 2, 4, "sim_unit", g, q, j)
            at(a + OFF_E + q + 1.25, 0, "mask", g, q)
        at(a + UG + 0.25, 5, "max_row", g)
        for c in range(CT):
            at(a + OFF_C + 4 + 2 * c, 5, "pv", g, c, 0)
            at(a + OFF_E + 4 + 2 * c, 5, "pv", g, c, 1)
        at(a + OFF_C + UG + 2, 1, "save", g, 0)
        at(a + OFF_E + UG + 2.75, 1, "save", g, 1)
        at(a + OFF_C + UG + 3.25, 5, "normalise", g, 0)
        at(a + OFF_E + UG + 4, 5, "normalise", g, 1)
    ev.sort(key=lambda e: (e[0], e[1]))
    return [(kind, args) for _, _, kind, args in ev]


EVENTS = schedule()
PSUM_KINDS = ("x_transpose", "q_proj", "k_proj", "v_proj", "max_unit", "max_row", "exp_unit", "normalise",
              "o_transpose", "proj_norm", "t_transpose", "sim_unit", "proj_out", "gate_transpose", "gate_logits")
UNIT = {ev: k for k, ev in enumerate(e for e in EVENTS if e[0] in PSUM_KINDS)}
SPLIT = {ev: k for k, ev in enumerate(e for e in EVENTS if e[0] in ("q_proj", "k_proj", "t_transpose"))}


def unit(kind, *args):
    return UNIT[(kind, args)]


def build(nc, ids, table, ln_scale, ln_bias, qkv_wt, qkv_b, proj_wt, proj_b, proj_wt_n, proj_b_n, gate_wt, w1, b1, w2, b2, out):
    ctx = ExitStack()
    with ctx:
        def sb(name, shape, dt=F32):
            return ctx.enter_context(nc.sbuf_tensor(name, shape, dt))

        def sem(name):
            return ctx.enter_context(nc.semaphore(name))

        x2_rows = nc.dram_tensor("x2_rows", (B * N, C), F32).ap()

        ident = sb("ident", [P, P])
        ids_sb = sb("ids_sb", [P, TILES], I32)
        rows_sb = sb("rows_sb", [P, TILES], I32)
        H = sb("H", [P, TILES, C])
        X = sb("X", [P, CT, C])
        X2 = sb("X2", [P, CT, C])
        scale_b = sb("scale_b", [P, C])
        bias_b = sb("bias_b", [P, C])
        stats = {name: sb(f"stats_{name}", [P, CT, 6]) for name in ("in", "out")}
        mv = sb("mv", [P, CT, 2])
        mv_x = sb("mv_x", [P, TILES, 2])
        rstd_x = sb("rstd_x", [P, TILES])
        nt = [sb(f"newton{i}", [P, CT * NH]) for i in range(4)]
        nt_in = [sb(f"newton_in{i}", [P, CT]) for i in range(4)]
        nt_out = [sb(f"newton_out{i}", [P, CT]) for i in range(4)]
        LG = sb("LG", [P, TILES, E])

        W1B = E * KC * HID
        arena1 = sb("arena1", [P, W1B])
        w1_sb = arena1[:, :].rearrange("p (e k h) -> p e k h", e=E, k=KC)
        at1 = [0]

        def carve(arena, pos, free):
            v = arena[:, pos[0]:pos[0] + free]
            pos[0] += free
            return v

        P1 = carve(arena1, at1, PRING * N).rearrange("p (s n) -> p s n", s=PRING)
        XT = carve(arena1, at1, KC * N).rearrange("p (k n) -> p k n", k=KC)
        WQKV = carve(arena1, at1, KC * 3 * C).rearrange("p (k m) -> p k m", k=KC)
        assert at1[0] <= W1B
        PART = KC * N // 2
        arena3 = sb("arena3", [P, 9 * PART + 2 * KC * N])
        PARTS = {nm: arena3[:, i * PART:(i + 1) * PART].bitcast(BF16).rearrange("p (k n) -> p k n", k=KC)
                 for i, nm in enumerate(r + part for r in "QKT" for part in "HML")}
        RESTS = 2 * KC
        REST = [arena3[:, 9 * PART + i * N:9 * PART + (i + 1) * N] for i in range(RESTS)]
        late_stacks = [sb(f"late_stacks{i}", [P, GH * N], BF16)[:, :] for i in range(SLOTS[0] + 1)]
        QS = [[carve(arena1, at1, GH * N // 2)[0:SD + 2].bitcast(BF16).rearrange("p (h n) -> p h n", h=GH) if i < 3
               else late_stacks[4][0:SD + 2].rearrange("p (h n) -> p h n", h=GH) for i in range(SLOTS[0])],
              [sb(f"QS1_{i}", [SD, GH, N], BF16)[:, :, :] for i in range(SLOTS[1])]]
        KS = [[late_stacks[i][0:SD + 2].rearrange("p (h n) -> p h n", h=GH) for i in range(SLOTS[0])],
              [sb(f"KS1_{i}", [SD, GH, N], BF16)[:, :, :] for i in range(SLOTS[1])]]
        assert at1[0] <= W1B
        w2_free = E * HC * C
        arena2 = sb("arena2", [P, B * CT * NH * VW + PRING * N + 2 * N])
        w2_sb = arena2[:, 0:w2_free].rearrange("p (e k d) -> p e k d", e=E, k=HC)
        at2 = [0]
        V = [carve(arena2, at2, CT * NH * VW).rearrange("p (c h w) -> p c h w", c=CT, h=NH) for _ in range(B)]
        P2 = carve(arena2, at2, PRING * N).rearrange("p (s n) -> p s n", s=PRING)
        ACCS = carve(arena2, at2, 2 * N).rearrange("p (s n) -> p s n", s=2)
        O = [sb(f"O{ps}", [P, CT, C]) for ps in range(2)]
        OT = sb("OT", [KW + 1, KC, N])
        T = sb("T", [P, CT, C])
        SQ = sb("SQ", [P, CT, C])
        PW = sb("PW", [KW + 1, KC, C])
        PWN = sb("PWN", [KW + 1, KC, C])
        GT = sb("GT", [KW, KC, E])
        MX = sb("MX", [P, 2, 4 * GH])
        MRH = sb("MRH", [4 * GH, 2, P], BF16)
        MRM = sb("MRM", [4 * GH, 2, P], BF16)
        rec = sb("rec", [P, CT, GH])

        x_flat, x_at = X[:, :, :].rearrange("p c d -> p (c d)"), [0]

        zeros = sb("zeros", [P, C])
        ones = sb("ones", [P, P])
        before = sb("before", [P, P])
        slot_no = sb("slot_no", [P, P])
        block_no = sb("block_no", [P, NBLK])
        expert_no = sb("expert_no", [P, TILES, E])
        not_first = sb("not_first", [P, E, TILES])
        dump_1 = sb("dump_1", [P, 1])
        rt = {nm: sb(f"rt_{nm}", [P, TILES, E]) for nm in ("a", "b", "oh0", "oh1", "prob")}
        col = {nm: sb(f"col_{nm}", [P, TILES]) for nm in ("m", "p0", "p1", "r")}
        weight = sb("weight", [P, TOPK, TILES])
        place = carve(x_flat, x_at, TOPK * TILES).rearrange("p (k t) -> p k t", k=TOPK)
        place_i = sb("place_i", [P, TOPK, TILES], I32)
        part_i = sb("part_i", [P, TOPK, TILES], I32)
        row_f = carve(x_flat, x_at, TOPK * TILES).rearrange("p (k t) -> p k t", k=TOPK)
        blk_f = carve(x_flat, x_at, TOPK * TILES).rearrange("p (k t) -> p k t", k=TOPK)
        exp8 = {nm: sb(f"exp8_{nm}", [P, E]) for nm in ("n", "end", "base")}
        exp8_i = sb("exp8_i", [P, E], I32)
        NQ = TOPK * TILES
        HQ = NQ // 2
        oh_blk = late_stacks[4][:, 0:NQ * NBLK].rearrange("p (q j) -> p q j", j=NBLK)
        tag = arena3[:, 0:NQ * NBLK].bitcast(BF16).rearrange("p (q s j) -> p q s j", s=2, j=NBLK)
        wtag = [late_stacks[2 + i][:, 0:HQ * 3 * NBLK].rearrange("p (q s j) -> p q s j", s=3, j=NBLK) for i in range(2)]
        oh_row = [late_stacks[i][:, 0:HQ * P].rearrange("p (q r) -> p q r", r=P) for i in range(2)]
        assert HQ * 3 * NBLK <= GH * N and NQ * NBLK <= GH * N
        token_i = sb("token_i", [P, TILES], I32)
        token_part = [sb(f"token_part{i}", [P, TILES]) for i in range(2)]
        weight_part = [sb(f"weight_part{i}", [P, NQ], BF16) for i in range(3)]
        weight_rest = sb("weight_rest", [P, NQ])
        slot_token = sb("slot_token", [P, NBLK], I32)
        slot_dest = sb("slot_dest", [P, NBLK], I32)
        slot_weight = carve(x_flat, x_at, NBLK)
        slot_tmp = carve(x_flat, x_at, NBLK)
        slot_dump = carve(x_flat, x_at, NBLK)
        blk_ge = carve(x_flat, x_at, NBLK * E)[0:1, :].rearrange("p (j e) -> p j e", e=E)
        blk_expert_f = carve(x_flat, x_at, NBLK)[0:1, :]
        blk_expert = sb("blk_expert", [1, NBLK], I32)
        at3 = [0]
        W1S = [carve(arena3, at3, KC * HID).rearrange("p (k h) -> p k h", k=KC) for _ in range(2)]
        HT = [carve(arena3, at3, HID).rearrange("p (k t) -> p k t", k=HC) for _ in range(2)]
        b2_b = carve(arena3, at3, E * C).rearrange("p (e d) -> p e d", e=E)
        XG = [T[:, i, :] for i in range(2)]
        XGT = [OT[:, :, i * P:(i + 1) * P] for i in range(2)]
        Y = [T[:, 2 + i, :] for i in range(2)]

        psum = ctx.enter_context(nc.psum_tensor("psum", [P, 8, N], F32))
        acc = [psum[:, 6, :], psum[:, 7, :]]

        def slot(k):
            return psum[:, k % RING, :]

        def slot_tiles(k):
            return psum[:, k % RING, 0:2 * C].rearrange("p (c d) -> p c d", c=2)

        hid_ps = [psum[:, 2 * i:2 * i + 2, :].rearrange("p b n -> p (b n)")[:, 0:HID] for i in range(2)]
        xgt_ps = [psum[0:KW, 4 + i, 0:KC * P].rearrange("p (k t) -> p k t", k=KC) for i in range(2)]
        y_ps = [psum[:, 6 + i, 0:C] for i in range(2)]

        ids_in, lnw_in, wqkv_in, pw_in, gt_in = (sem(s) for s in ("ids_in", "lnw_in", "wqkv_in", "pw_in", "gt_in"))
        ident_set, consts_set, ones_set, stack_ones_set, rows_ready = (
            sem(x) for x in ("ident_set", "consts_set", "ones_set", "stack_ones_set", "rows_ready"))
        gathered = [sem(f"gathered{b}") for b in range(B)]
        filled = [sem(f"psum_filled{s}") for s in range(RING)]
        freed = [sem(f"psum_freed{s}") for s in range(RING)]
        hi_written, mid_written, lo_written, row_hi = (sem(x) for x in ("hi_written", "mid_written", "lo_written", "row_hi"))
        x_ready = sem("x_ready")
        pool_step = sem("pool_step")
        qk_loaded = {x: [sem(f"{x}_loaded{s}") for s in range(SLOTS[0])] for x in "qk"}
        row_loaded = [sem(f"row_loaded{s}") for s in range(SLOTS[0])]
        sim_loaded = {x: [sem(f"sim_{x}_loaded{s}") for s in range(SLOTS[1])] for x in "qk"}
        pv_done = [sem("pv1_done"), sem("pv2_done")]
        acc_saved = [sem("acc1_saved"), sem("acc2_saved")]
        masked = sem("masked")
        sq_done, t_ready, x2_ready = sem("sq_done"), sem("t_ready"), sem("x2_ready")
        x2_stored, h_stored = sem("x2_stored"), sem("h_stored")
        dve_step = sem("dve_step")
        iotas_set, zeros_set = sem("iotas_set"), sem("zeros_set")
        w1_in, w2_in, b2_in, dump_in = sem("w1_in"), sem("w2_in"), sem("b2_in"), sem("dump_in")
        shifted, exped, chosen, counted = sem("logits_shifted"), sem("logits_exped"), sem("experts_chosen"), sem("tokens_counted")
        tags_ready, row_ready, listed = sem("tags_ready"), sem("row_ready"), sem("slots_listed")
        wtags_ready, weights_listed, weights_ready = sem("wtags_ready"), sem("weights_listed"), sem("weights_ready")
        lists_ready = sem("lists_ready")
        xg_loaded = [sem(f"xg_loaded{i}") for i in range(2)]
        xgt_filled, xgt_ready, w1_staged = sem("xgt_filled"), sem("xgt_ready"), sem("w1_staged")
        hid_filled, hid_done, y_filled = sem("hid_filled"), sem("hid_done"), sem("y_filled")
        y_biased, y_weighted, scattered = sem("y_biased"), sem("y_weighted"), sem("scattered")

        def wait_filled(e, k):
            e.wait_ge(filled[k % RING], k // RING + 1)

        def wait_consumed(e, k):
            e.wait_ge(freed[k % RING], k // RING + 1)

        def part_rows(nm, g):
            return PARTS[nm][GC * (g % 2):GC * (g % 2) + GC, 0, :] if g < 2 else PARTS[nm][GC:2 * GC, 1, :]

        LOADS = 16 * len(Q_PARTS)

        def lo_part(eng, source, b, j):
            n = SPLIT[(source, (b, j))]
            part = source[0].upper()
            eng.wait_ge(mid_written, n + 1)
            eng.tensor_tensor(PARTS[part + "L"][:, j, :], REST[n % RESTS], PARTS[part + "M"][:, j, :], ALU.subtract).then_inc(lo_written, 1)

        def load_part(eng, g, r, ps, dst, role, parts, source, done):
            n = SPLIT[(source, (g // GB, 1))]
            eng.wait_ge({"H": hi_written, "M": mid_written, "L": lo_written}[parts[r]], n + 1)
            last_reader = ("exp_unit", "sim_unit")[ps]
            if g >= SLOTS[ps]:
                wait_filled(eng, unit(last_reader, g - SLOTS[ps], UG - 1, 1))
            eng.dma_start(dst[g % SLOTS[ps]][r * D:(r + 1) * D, :, :].rearrange("d h n -> d (h n)"),
                          part_rows(role + parts[r], g % GB)).then_inc(done[g % SLOTS[ps]], 16)

        def wait_past(e, s_, v):
            if not isinstance(v, int) or v > 0:
                e.wait_ge(s_, v)

        def over_blocks(eng, step):
            tail = 3
            step(0, 0)
            step(1, 1)
            with eng.Fori(1, (NBLK - tail) // 2) as pair:
                for i in range(2):
                    step(2 * pair + i, i)
            for j in range(NBLK - tail, NBLK):
                step(j, j % 2)

        with nc.Block() as block:

            @block.sync
            def _(sp):
                sp.dma_start(ids_sb[:, :].rearrange("p (b c) -> p b c", b=B),
                             ids.rearrange("b (p c) -> p b c", c=CT)).then_inc(ids_in, 16)
                sp.dma_start(scale_b[:, :], ln_scale.partition_broadcast(P)).then_inc(lnw_in, 16)
                sp.dma_start(bias_b[:, :], ln_bias.partition_broadcast(P)).then_inc(lnw_in, 16)
                sp.dma_start(WQKV[0:KW], qkv_wt.rearrange("(k p) m -> p k m", k=KC)).then_inc(wqkv_in, 16)
                sp.dma_start(WQKV[KW:KW + 1, 0, :], qkv_b.unsqueeze(0)).then_inc(wqkv_in, 16)
                sp.dma_start(PW[0:KW], proj_wt.rearrange("(k p) m -> p k m", k=KC)).then_inc(pw_in, 16)
                sp.dma_start(PW[KW:KW + 1, 0, :], proj_b.unsqueeze(0)).then_inc(pw_in, 16)
                sp.dma_start(PWN[0:KW], proj_wt_n.rearrange("(k p) m -> p k m", k=KC)).then_inc(pw_in, 16)
                sp.dma_start(PWN[KW:KW + 1, 0, :], proj_b_n.unsqueeze(0)).then_inc(pw_in, 16)
                sp.dma_start(GT[:, :, :], gate_wt.rearrange("(k p) e -> p k e", k=KC)).then_inc(gt_in, 16)

                for kind, args in EVENTS:
                    if kind == "load_qk":
                        g, r = args
                        load_part(sp, g, Q_ORDER[r], 0, QS[0], "Q", Q_PARTS, "q_proj", qk_loaded["q"])
                    elif kind == "max_row":
                        g, = args
                        wait_consumed(sp, unit("max_row", g))
                        for r, m in enumerate((MRH, MRM)):
                            sp.dma_start(QS[0][g % SLOTS[0]][SD + r:SD + r + 1, :, :].rearrange("o h n -> o (h n)"),
                                         m[:, g % 2, :]).then_inc(row_loaded[g % SLOTS[0]], 16)
                    elif kind == "load_sim":
                        g, r = args
                        load_part(sp, g, Q_ORDER[r], 1, QS[1], "T", Q_PARTS, "t_transpose", sim_loaded["q"])
                        if args == (NG - 1, len(Q_PARTS) - 1):
                            sp.wait_ge(pv_done[0], CT * NG)
                            for e in range(E):
                                sp.dma_start(w1_sb[0:KW, e], w1[e].rearrange("(k p) h -> p k h", k=KC)).then_inc(w1_in, 16)
                            sp.dma_start(w1_sb[KW:KW + 1, :, 0, :], b1.unsqueeze(0)).then_inc(w1_in, 16)
                            sp.wait_ge(zeros_set, 1)
                            sp.dma_start(out[DUMP:DUMP + P, :], zeros[:, :]).then_inc(dump_in, 16)
                    elif kind == "normalise" and args == (NG - 1, 1):
                        wait_filled(sp, unit("normalise", NG - 1, 1))
                        sp.wait_ge(pv_done[0], CT * NG)
                        for e in range(E):
                            sp.dma_start(w2_sb[:, e], w2[e].rearrange("(k p) d -> p k d", p=P)).then_inc(w2_in, 16)
                    elif kind == "out_norm" and args[1] == "apply":
                        b = args[0]
                        sp.wait_ge(x2_ready, b + 1)
                        rows = slice(b * N, (b + 1) * N)
                        sp.dma_start(x2_rows[rows, :].rearrange("(p c) d -> p c d", c=CT), X2[:, :, :]).then_inc(x2_stored, 16)
                        sp.dma_start(out[rows, :].rearrange("(p c) d -> p c d", c=CT),
                                     H[:, CT * b:CT * (b + 1), :]).then_inc(h_stored, 16)
                sp.wait_ge(lists_ready, 1)
                sp.dma_start(b2_b, b2.partition_broadcast(P)).then_inc(b2_in, 16)
                sp.wait_ge(scattered, 16 * NBLK)

            @block.gpsimd
            def _(pool):
                pool.memset(ident[:, :], 0.0).then_inc(pool_step, 1)
                pool.wait_ge(pool_step, 1)
                pool.affine_select(out=ident[:, :], in_=ident[:, :], compare_op=ALU.not_equal, fill=1.0, base=0,
                                   pattern=[[-1, P]], channel_multiplier=1).then_inc(ident_set, 1)
                pool.wait_ge(rows_ready, 1)
                for t in range(TILES):
                    pool.indirect_dma_start(H[:, t, :], None, table,
                                            bass.IndirectOffsetOnAxis(ap=rows_sb[:, t:t + 1], axis=0)
                                            ).then_inc(gathered[t // CT], 16)
                pool.wait_ge(ident_set, 1)
                for n in range(SLOTS[0]):
                    pool.memset(KS[0][n][SD:SD + 2, :, :], 1.0).then_inc(stack_ones_set, 1)
                    pool.wait_ge(stack_ones_set, n + 1)
                any_dt = dict(allow_small_or_imprecise_dtypes=True)
                pool.memset(zeros[:, :], 0.0).then_inc(zeros_set, 1)
                pool.memset(ones[:, :], 1.0).then_inc(pool_step, 1)
                pool.memset(not_first[:, :, :], 1.0).then_inc(pool_step, 1)
                pool.iota(slot_no[:, :], pattern=[[1, P]], base=0, channel_multiplier=0, **any_dt)
                pool.iota(block_no[:, :], pattern=[[1, NBLK]], base=0, channel_multiplier=0, **any_dt)
                pool.iota(expert_no[:, :, :], pattern=[[0, TILES], [1, E]], base=0, channel_multiplier=0, **any_dt)
                pool.iota(token_i[:, :].rearrange("p (b c) -> p b c", b=B), pattern=[[N, B], [1, CT]], base=0,
                          channel_multiplier=CT, **any_dt)
                pool.iota(dump_1[:, :], pattern=[[0, 1]], base=DUMP + 1, channel_multiplier=1, **any_dt)
                pool.wait_ge(pool_step, 3)
                pool.affine_select(out=before[:, :], in_=ones[:, :], compare_op=ALU.is_gt, fill=0.0, base=0,
                                   pattern=[[1, P]], channel_multiplier=-1)
                pool.affine_select(out=not_first[:, :, :], in_=not_first[:, :, :], compare_op=ALU.is_gt, fill=0.0, base=0,
                                   pattern=[[0, E], [1, TILES]], channel_multiplier=0).then_inc(iotas_set, 1)
                for kind, args in EVENTS:
                    if kind == "mid":
                        if args[1] > 0 or args[0] == "t_transpose":
                            lo_part(pool, *args)
                    elif kind == "load_qk":
                        load_part(pool, args[0], K_ORDER[args[1]], 0, KS[0], "K", K_PARTS, "k_proj", qk_loaded["k"])
                    elif kind == "load_sim":
                        load_part(pool, args[0], K_ORDER[args[1]], 1, KS[1], "T", K_PARTS, "t_transpose", sim_loaded["k"])

                def gather(j):
                    if j >= 2:
                        pool.wait_ge(xgt_filled, j - 1)
                    pool.indirect_dma_start(XG[j % 2], None, x2_rows,
                                            bass.IndirectOffsetOnAxis(ap=slot_token[:, j:j + 1], axis=0)
                                            ).then_inc(xg_loaded[j % 2], 16)

                pool.wait_ge(lists_ready, 1)
                pool.wait_ge(x2_stored, 16 * B)
                for j in range(3):
                    gather(j)
                pool.wait_ge(h_stored, 16 * B)
                pool.wait_ge(dump_in, 16)
                for j in range(NBLK):
                    if j + 3 < NBLK:
                        gather(j + 3)
                    pool.wait_ge(y_weighted, j + 1)
                    if j >= 1:
                        pool.wait_ge(scattered, 16 * j)
                    pool.indirect_dma_start(out, bass.IndirectOffsetOnAxis(ap=slot_dest[:, j:j + 1], axis=0), Y[j % 2], None,
                                            compute_op=ALU.add).then_inc(scattered, 16)

            @block.scalar
            def _(act):
                for kind, args in EVENTS:
                    if kind not in PSUM_KINDS and kind not in ("save", "mid"):
                        continue
                    if kind == "mid":
                        n = SPLIT[(args[0], args[1:])]
                        wait_consumed(act, unit(*args))
                        act.activation(PARTS[args[0][0].upper() + "M"][:, args[2], :], REST[n % RESTS], ACT.Copy).then_inc(mid_written, 1)
                        continue
                    if kind == "save":
                        g, ps = args
                        act.wait_ge(pv_done[ps], CT * (g + 1))
                        if g >= 1:
                            wait_filled(act, unit("normalise", g - 1, ps))
                        act.activation(ACCS[:, ps, :], acc[ps], ACT.Copy).then_inc(acc_saved[ps], 1)
                        continue
                    k = unit(kind, *args)
                    done = freed[k % RING]
                    s = slot(k)
                    if kind == "x_transpose":
                        b, j = args
                        wait_filled(act, k)
                        if b >= 1:
                            wait_filled(act, unit("v_proj", b - 1, 1))
                        act.activation(XT[0:KW, j, :], s[0:KW], ACT.Copy).then_inc(done, 1)
                    elif kind in ("q_proj", "k_proj", "t_transpose"):
                        b, j = args
                        wait_filled(act, k)
                        if b >= 1:
                            loaded = {"q_proj": [qk_loaded["q"]], "k_proj": [qk_loaded["k"]],
                                      "t_transpose": [sim_loaded["q"], sim_loaded["k"]]}[kind]
                            for side in loaded:
                                for g in range(max(0, GB * b - len(side)), GB * b):
                                    act.wait_ge(side[g % len(side)], LOADS * (g // len(side) + 1))
                        act.activation(PARTS[kind[0].upper() + "H"][:, j, :], s, ACT.Copy).then_inc(hi_written, 1)
                    elif kind == "v_proj":
                        b, j = args
                        wait_filled(act, k)
                        act.activation(V[b][:, 2 * j:2 * j + 2, :, 0:D],
                                       slot_tiles(k).rearrange("p c (h d) -> p c h d", d=D), ACT.Copy).then_inc(done, 1)
                    elif kind == "max_row":
                        g, = args
                        wait_filled(act, k)
                        if g >= 2:
                            act.wait_ge(row_loaded[(g - 2) % SLOTS[0]], 32 * ((g - 2) // SLOTS[0] + 1))
                        act.activation(MRH[:, g % 2, :], s[0:4 * GH, 0:P], ACT.Copy, scale=-1.0).then_inc(row_hi, 1)
                    elif kind in ("exp_unit", "sim_unit"):
                        g, q, j = args
                        n = 2 * (UG * g + q) + j
                        ps = int(kind == "sim_unit")
                        wait_filled(act, k)
                        if n >= PRING:
                            act.wait_ge(pv_done[ps], (n - PRING) // GH + 1)
                        act.activation((P1, P2)[ps][:, n % PRING, :], s, ACT.Exp,
                                       scale=(QSCALE, SIM_SCALE)[ps]).then_inc(done, 1)
                    elif kind in ("o_transpose", "gate_transpose"):
                        wait_filled(act, k)
                        for reader, j in (("proj_norm", 1), ("proj_out", 1)):
                            before_k = [unit(reader, n, j) for n in range(B) if unit(reader, n, j) < k]
                            if before_k:
                                wait_filled(act, max(before_k))
                        before_k = [unit("gate_logits", n) for n in range(B) if unit("gate_logits", n) < k]
                        if before_k:
                            wait_filled(act, max(before_k))
                        act.activation(OT[0:KW, args[-1], :], s[0:KW], ACT.Copy).then_inc(done, 1)
                    elif kind == "proj_norm":
                        wait_filled(act, k)
                        b, j = args
                        if b >= 1:
                            wait_filled(act, unit("t_transpose", b - 1, 1))
                        if b >= 1:
                            act.wait_ge(t_ready, b)
                        act.activation(SQ[:, 2 * j:2 * j + 2, :], slot_tiles(k), ACT.Square).then_inc(sq_done, 1)
                        act.activation(T[:, 2 * j:2 * j + 2, :], slot_tiles(k), ACT.Copy).then_inc(done, 1)

                act.wait_ge(shifted, 1)
                act.activation(rt["b"][:, :, :], rt["a"][:, :, :], ACT.Exp).then_inc(exped, 1)

                def step(j, i):
                    act.wait_ge(hid_filled, j + 1)
                    wait_past(act, y_filled, j - 1)
                    act.activation(HT[i].rearrange("p k t -> p (k t)"), hid_ps[i], ACT.Gelu).then_inc(hid_done, 1)

                over_blocks(act, step)

            @block.vector
            def _(dve):
                steps = [0]

                def link(ins):
                    steps[0] += 1
                    ins.then_inc(dve_step, 1)
                    dve.wait_ge(dve_step, steps[0])

                def rsqrt_op(i, tiles, dst, src, floor, add):
                    n = dst.shape[1]
                    x, y, t = (tile[:, 0:n] for tile in tiles[0:3])
                    if i == 0:
                        return dve.tensor_scalar(x, src, floor, add, ALU.max, ALU.add)
                    if i == 1:
                        return dve.tensor_scalar(t.bitcast(I32), x.bitcast(I32), 1, None, ALU.arith_shift_right)
                    if i == 2:
                        return dve.tensor_scalar(y.bitcast(I32), t.bitcast(I32), -1.0, float(RSQRT_MAGIC), ALU.mult, ALU.add)
                    if i % 3 == 0:
                        return dve.tensor_tensor(t, y, y, ALU.mult)
                    if i % 3 == 1:
                        return dve.scalar_tensor_tensor(t, t, -0.5, x, ALU.mult, ALU.mult)
                    return dve.scalar_tensor_tensor(dst if i == RSQRT_OPS - 1 else y, t, 1.5, y, ALU.add, ALU.mult)

                chain_at = {}

                def chain(name, ins):
                    steps[0] += 1
                    chain_at[name] = steps[0]
                    ins.then_inc(dve_step, 1)

                def norm_part(name, part, mean_var, tiles, rstd, src, eps):
                    if part == "stats":
                        for c in range(CT):
                            last = dve.bn_stats(stats[name][:, c, :], src[:, c, :])
                    elif part == "moments":
                        dve.wait_ge(dve_step, chain_at[name])
                        for c in range(CT):
                            last = dve.bn_aggr(mean_var[:, c, :], stats[name][:, c, :])
                    else:
                        dve.wait_ge(dve_step, chain_at[name])
                        last = rsqrt_op(part, tiles, rstd, mean_var[:, 0:CT, 1], 0.0, eps)
                    chain(name, last)

                def norm_apply(dst, src, mean_var, rstd):
                    for c in range(src.shape[1]):
                        last = dve.tensor_scalar(dst[:, c, :], src[:, c, :], mean_var[:, c, 0:1], rstd[:, c:c + 1],
                                                 ALU.subtract, ALU.mult)
                    return last

                dve.wait_ge(ids_in, 16)
                dve.tensor_scalar(rows_sb[:, :], ids_sb[:, :], BUCKETS - 1, None, ALU.bitwise_and).then_inc(rows_ready, 1)
                dve.memset(XT[KW:KW + 1, 0, :], 1.0)
                dve.memset(OT[KW:KW + 1, 0, :], 1.0).then_inc(consts_set, 1)

                for kind, args in EVENTS:
                    k = unit(kind, *args) if kind in PSUM_KINDS else None
                    if kind == "embed_norm":
                        b, part = args
                        tiles = slice(CT * b, CT * (b + 1))
                        h, moments, rstd = H[:, tiles, :], mv_x[:, tiles, :], rstd_x[:, tiles]
                        if part == "stats":
                            dve.wait_ge(gathered[b], 16 * CT)
                        if part == "apply":
                            dve.wait_ge(dve_step, chain_at["in"])
                            chain("in", norm_apply(h, h, moments, rstd))
                        elif part in ("scale", "bias"):
                            dve.wait_ge(dve_step, chain_at["in"])
                            dve.wait_ge(lnw_in, 32)
                            w, op = {"scale": (scale_b, ALU.mult), "bias": (bias_b, ALU.add)}[part]
                            chain("in", dve.tensor_tensor(h, h, w[:, :].unsqueeze(1).to_broadcast([P, CT, C]), op))
                        else:
                            norm_part("in", part, moments, nt_in, rstd, h, 1e-6)
                    elif kind == "attn_stats":
                        b, part = args
                        tiles = slice(CT * b, CT * (b + 1))
                        if part == "stats":
                            dve.wait_ge(dve_step, chain_at["in"])
                        norm_part("in", part, mv_x[:, tiles, :], nt_in, rstd_x[:, tiles], H[:, tiles, :], 1e-5)
                    elif kind == "attn_norm":
                        b, = args
                        tiles = slice(CT * b, CT * (b + 1))
                        dve.wait_ge(dve_step, chain_at["in"])
                        if b >= 1:
                            wait_filled(dve, unit("x_transpose", b - 1, 1))
                        if b == 1:
                            dve.wait_ge(iotas_set, 1)
                            link(dve.tensor_scalar(part_i[:, 0, :], token_i[:, :], B * N - P, None, ALU.bitwise_and))
                            link(dve.tensor_scalar(part_i[:, 1, :], token_i[:, :], P - 1, None, ALU.bitwise_and))
                            dve.tensor_copy(token_part[0][:, :], part_i[:, 0, :])
                            link(dve.tensor_scalar(token_part[1][:, :], part_i[:, 1, :], 1.0, None, ALU.add))
                        norm_apply(X, H[:, tiles, :], mv_x[:, tiles, :], rstd_x[:, tiles]).then_inc(x_ready, 1)
                        if b == 0:
                            dve.memset(acc[0], 0.0)
                            dve.memset(acc[1], 0.0)
                            for n in range(B):
                                last = dve.memset(V[n][:, :, :, D:VW], 1.0)
                            last.then_inc(ones_set, 1)
                    elif kind == "mid":
                        if args[1] == 0 and args[0] != "t_transpose":
                            lo_part(dve, *args)
                    elif kind in ("q_proj", "k_proj", "t_transpose"):
                        n = SPLIT[(kind, args)]
                        dve.wait_ge(hi_written, n + 1)
                        if n >= RESTS:
                            dve.wait_ge(lo_written, n - RESTS + 1)
                        dve.tensor_tensor(REST[n % RESTS], slot(k), PARTS[kind[0].upper() + "H"][:, args[1], :], ALU.subtract).then_inc(freed[k % RING], 1)
                    elif kind == "max_unit":
                        g, q, j = args
                        i, c = (2 * q + j) % GH, q // 2
                        if q == 0 and j == 0 and g >= 2:
                            wait_filled(dve, unit("max_row", g - 2))
                        wait_filled(dve, k)
                        dve.tensor_reduce(MX[:, g % 2, CT * i + c:CT * i + c + 1], slot(k), AX_X, ALU.max
                                          ).then_inc(freed[k % RING], 1)
                    elif kind == "max_row":
                        g, = args
                        dve.wait_ge(row_hi, g + 1)
                        dve.scalar_tensor_tensor(MRM[:, g % 2, :], slot(k)[0:4 * GH, 0:P], -1.0,
                                                 MRH[:, g % 2, :], ALU.mult, ALU.subtract
                                                 ).then_inc(freed[k % RING], 1)
                    elif kind == "mask":
                        g, q = args
                        wait_consumed(dve, unit("sim_unit", g, q, 0))
                        wait_consumed(dve, unit("sim_unit", g, q, 1))
                        n = 2 * (UG * g + q) % PRING
                        p = P2[:, n:n + 2, :]
                        dve.scalar_tensor_tensor(p, p, 1.0, p, ALU.is_ge, ALU.mult).then_inc(masked, 1)
                    elif kind == "normalise":
                        g, ps = args
                        wait_filled(dve, k)
                        v = slot(k).rearrange("p (c h w) -> p c h w", c=CT, h=GH)
                        link(dve.reciprocal(rec[:, :, :], v[:, :, :, D]))
                        if g % GB == 0:
                            if g >= GB:
                                wait_filled(dve, unit("o_transpose", g // GB - 1, ps, 1))
                        o = O[ps][:, :, (g % GB) * GH * D:(g % GB + 1) * GH * D].rearrange("p c (h d) -> p c h d", d=D)
                        dve.tensor_tensor(o, v[:, :, :, 0:D], rec[:, :, :].unsqueeze(3).to_broadcast([P, CT, GH, D]),
                                          ALU.mult).then_inc(freed[k % RING], 1)
                    elif kind == "unit_tokens":
                        b, part = args
                        ss = nt[3][:, 0:CT * NH]
                        if part == "squares":
                            dve.wait_ge(sq_done, 2 * (b + 1))
                            squares = SQ[:, :, :].rearrange("p c (g d h) -> p (c g) d h", g=GB, h=GH)
                            chain("unit", dve.tensor_reduce(ss, squares.rearrange("p x d h -> p x h d"), AX_X, ALU.add))
                        elif part == "scale":
                            dve.wait_ge(dve_step, chain_at["unit"])
                            wait_consumed(dve, unit("proj_norm", b, 0))
                            wait_consumed(dve, unit("proj_norm", b, 1))
                            tiles = T[:, :, :].rearrange("p c (g d h) -> p (c g) d h", g=GB, h=GH)
                            dve.tensor_tensor(tiles, tiles, ss.rearrange("p (x h) -> p x h", h=GH).unsqueeze(2).to_broadcast(
                                [P, CT * GB, D, GH]), ALU.mult).then_inc(t_ready, 1)
                        else:
                            dve.wait_ge(dve_step, chain_at["unit"])
                            chain("unit", rsqrt_op(part, nt, ss, ss, 1e-24, 0.0))
                    elif kind == "proj_out":
                        b, j = args
                        h = H[:, CT * b + 2 * j:CT * b + 2 * j + 2, :]
                        wait_filled(dve, k)
                        dve.tensor_tensor(h, slot_tiles(k), h, ALU.add).then_inc(freed[k % RING], 1)
                    elif kind == "out_norm":
                        b, part = args
                        h = H[:, CT * b:CT * (b + 1), :]
                        rstd = nt_out[3][:, :]
                        if part == "apply":
                            dve.wait_ge(dve_step, chain_at["out"])
                            if b >= 1:
                                dve.wait_ge(x2_stored, 16 * b)
                                wait_filled(dve, unit("gate_transpose", b - 1, 1))
                            norm_apply(X2, h, mv, rstd).then_inc(x2_ready, 1)
                        else:
                            if part == "stats":
                                for j in range(2):
                                    wait_consumed(dve, unit("proj_out", b, j))
                            norm_part("out", part, mv, nt_out, rstd, h, 1e-5)
                    elif kind == "gate_logits":
                        b, = args
                        wait_filled(dve, k)
                        dve.tensor_copy(LG[:, CT * b:CT * (b + 1), :],
                                        slot(k)[:, 0:CT * E].rearrange("p (c e) -> p c e", e=E)).then_inc(freed[k % RING], 1)

                def per_expert(v):
                    return v.unsqueeze(2).to_broadcast([P, TILES, E])

                a, bb, prob = rt["a"][:, :, :], rt["b"][:, :, :], rt["prob"][:, :, :]
                m, r = col["m"][:, :], col["r"][:, :]
                wait_consumed(dve, unit("gate_logits", B - 1))
                dve.wait_ge(iotas_set, 1)
                link(dve.tensor_reduce(m, LG[:, :, :], AX_X, ALU.max))
                dve.tensor_tensor(a, LG[:, :, :], per_expert(m), ALU.subtract).then_inc(shifted, 1)
                dve.wait_ge(exped, 1)
                link(dve.tensor_reduce(m, bb, AX_X, ALU.add))
                link(dve.reciprocal(r, m))
                link(dve.tensor_tensor(prob, bb, per_expert(r), ALU.mult))
                for n in range(TOPK):
                    top, oh = col[f"p{n}"][:, :], rt[f"oh{n}"][:, :, :]
                    link(dve.tensor_reduce(top, prob, AX_X, ALU.max))
                    link(dve.tensor_tensor(a, prob, per_expert(top), ALU.is_equal))
                    link(dve.scalar_tensor_tensor(a, a, -float(E), expert_no[:, :, :], ALU.mult, ALU.add))
                    link(dve.tensor_reduce(m, a, AX_X, ALU.min))
                    link(dve.tensor_tensor(oh, a, per_expert(m), ALU.is_equal))
                    if n == 0:
                        link(dve.scalar_tensor_tensor(prob, oh, -4.0, prob, ALU.mult, ALU.add))
                oh0, oh1 = rt["oh0"][:, :, :], rt["oh1"][:, :, :]
                dve.tensor_tensor(bb, oh0, oh1, ALU.add).then_inc(chosen, 1)
                link(dve.scalar_tensor_tensor(m, col["p0"][:, :], 1e-9, col["p1"][:, :], ALU.add, ALU.add))
                link(dve.reciprocal(r, m))
                for n in range(TOPK):
                    dve.tensor_tensor(weight[:, n, :], col[f"p{n}"][:, :], r, ALU.mult)
                dve.wait_ge(counted, 1)
                tot, inc = a.rearrange("p t e -> p (t e)").rearrange("p (e t) -> p e t", e=E), prob.rearrange("p t e -> p (t e)").rearrange("p (e t) -> p e t", e=E)
                link(dve.tensor_copy(tot, psum[:, 1, 0:P].rearrange("p (t e) -> p e t", e=E)))
                link(dve.tensor_tensor_scan(prob.rearrange("p t e -> p (t e)"), not_first[:, :, :].rearrange("p e t -> p (e t)"),
                                            a.rearrange("p t e -> p (t e)"), 0.0, ALU.mult, ALU.add))
                cnt, end, base = (exp8[nm][:, :] for nm in ("n", "end", "base"))
                link(dve.tensor_scalar(exp8_i[:, :], inc[:, :, TILES - 1], float(P - 1), None, ALU.add))
                link(dve.tensor_scalar(exp8_i[:, :], exp8_i[:, :], P.bit_length() - 1, None, ALU.arith_shift_right))
                link(dve.tensor_copy(cnt, exp8_i[:, :]))
                link(dve.tensor_tensor_scan(end, ones[:, 0:E], cnt, 0.0, ALU.mult, ALU.add))
                link(dve.tensor_tensor(base, end, cnt, ALU.subtract))
                link(dve.tensor_tensor(inc, inc, tot, ALU.subtract))
                link(dve.scalar_tensor_tensor(inc, base.unsqueeze(2).to_broadcast([P, E, TILES]), float(P), inc, ALU.mult, ALU.add))
                link(dve.tensor_tensor(bb, psum[:, 0, 0:P].rearrange("p (t e) -> p t e", e=E), inc.rearrange("p e t -> p t e"), ALU.add))
                for n in range(TOPK):
                    link(dve.tensor_tensor(a, bb, rt[f"oh{n}"][:, :, :], ALU.mult))
                    link(dve.tensor_reduce(place[:, n, :], a, AX_X, ALU.add))
                link(dve.tensor_copy(place_i[:, :, :], place[:, :, :]))
                link(dve.tensor_scalar(part_i[:, :, :], place_i[:, :, :], P - 1, None, ALU.bitwise_and))
                link(dve.tensor_copy(row_f[:, :, :], part_i[:, :, :]))
                link(dve.tensor_scalar(part_i[:, :, :], place_i[:, :, :], P.bit_length() - 1, None, ALU.arith_shift_right))
                link(dve.tensor_copy(blk_f[:, :, :], part_i[:, :, :]))
                blk = blk_f[:, :, :].rearrange("p n t -> p (n t)")
                link(dve.tensor_tensor(oh_blk, block_no[:, :].unsqueeze(1).to_broadcast([P, NQ, NBLK]),
                                       blk.unsqueeze(2).to_broadcast([P, NQ, NBLK]), ALU.is_equal))
                for n in range(TOPK):
                    for i in range(2):
                        last = dve.tensor_tensor(tag[:, n * TILES:(n + 1) * TILES, i, :], oh_blk[:, n * TILES:(n + 1) * TILES, :],
                                                 token_part[i][:, :].unsqueeze(2).to_broadcast([P, TILES, NBLK]), ALU.mult)
                last.then_inc(tags_ready, 1)
                rows = row_f[:, :, :].rearrange("p n t -> p (n t)")
                for q in range(NQ):
                    dve.tensor_scalar(oh_row[q // HQ][:, q % HQ, :], slot_no[:, :], rows[:, q:q + 1], None, ALU.is_equal).then_inc(row_ready, 1)
                link(dve.tensor_tensor(blk_ge, block_no[0:1, :].unsqueeze(2).to_broadcast([1, NBLK, E]),
                                       end[0:1, :].unsqueeze(1).to_broadcast([1, NBLK, E]), ALU.is_ge))
                link(dve.tensor_reduce(blk_expert_f[:, :], blk_ge, AX_X, ALU.add))
                dve.tensor_scalar(blk_expert[:, :], blk_expert_f[:, :], float(E - 1), None, ALU.min)
                dve.wait_ge(listed, 1)
                tok = slot_tmp
                link(dve.tensor_copy(slot_weight[:, :], psum[:, 2, NBLK:2 * NBLK]))
                link(dve.tensor_tensor(tok, psum[:, 2, 0:NBLK], slot_weight[:, :], ALU.add))
                dve.tensor_scalar(slot_token[:, :], tok, -1.0, 0.0, ALU.add, ALU.max)
                link(dve.tensor_scalar(slot_dump, tok, 0.0, dump_1[:, 0:1], ALU.is_equal, ALU.mult))
                dve.scalar_tensor_tensor(slot_dest[:, :], tok, -1.0, slot_dump, ALU.add, ALU.add).then_inc(lists_ready, 1)
                dve.wait_ge(lists_ready, 1)

                def weigh_slots():
                    w = weight[:, :, :].rearrange("p n t -> p (n t)")
                    link(dve.tensor_copy(weight_part[0][:, :], w))
                    link(dve.tensor_tensor(weight_rest[:, :], w, weight_part[0][:, :], ALU.subtract))
                    link(dve.tensor_copy(weight_part[1][:, :], weight_rest[:, :]))
                    link(dve.tensor_tensor(weight_part[2][:, :], weight_rest[:, :], weight_part[1][:, :], ALU.subtract))
                    for h in range(2):
                        for i in range(3):
                            dve.tensor_tensor(wtag[h][:, :, i, :], oh_blk[:, h * HQ:(h + 1) * HQ, :],
                                              weight_part[i][:, h * HQ:(h + 1) * HQ].unsqueeze(2).to_broadcast([P, HQ, NBLK]),
                                              ALU.mult).then_inc(wtags_ready, 1)

                def gather_weights():
                    dve.wait_ge(weights_listed, 1)
                    parts = psum[:, 7, 0:3 * NBLK]
                    link(dve.tensor_copy(slot_weight[:, :], parts[:, 2 * NBLK:3 * NBLK]))
                    link(dve.tensor_tensor(slot_weight[:, :], parts[:, NBLK:2 * NBLK], slot_weight[:, :], ALU.add))
                    dve.tensor_tensor(slot_weight[:, :], parts[:, 0:NBLK], slot_weight[:, :], ALU.add).then_inc(weights_ready, 1)
                    dve.wait_ge(weights_ready, 1)

                def stage(j, i):
                    e = dve.value_load(blk_expert[0:1, bass.ds(j, 1)], min_val=0, max_val=E - 1)
                    wait_past(dve, hid_filled, j - 1)
                    dve.tensor_copy(W1S[i][0:KW, 1, :], w1_sb[0:KW, bass.ds(e, 1), 1, :].rearrange("p o h -> p (o h)"))
                    dve.tensor_copy(W1S[i][0:KW + 1, 0, :], w1_sb[0:KW + 1, bass.ds(e, 1), 0, :].rearrange("p o h -> p (o h)")).then_inc(w1_staged, 1)

                def take_tokens(j, i):
                    dve.wait_ge(xgt_filled, j + 1)
                    dve.tensor_copy(XGT[i][0:KW, :, :], xgt_ps[i]).then_inc(xgt_ready, 1)

                def step(j, i):
                    if not isinstance(j, int) or j + 2 < NBLK:
                        stage(j + 2, i)
                        take_tokens(j + 2, i)
                    e = dve.value_load(blk_expert[0:1, bass.ds(j, 1)], min_val=0, max_val=E - 1)
                    dve.wait_ge(y_filled, j + 1)
                    wait_past(dve, scattered, 16 * (j - 1))
                    dve.tensor_tensor(Y[i], y_ps[i], b2_b[:, bass.ds(e, 1), :].rearrange("p o d -> p (o d)"), ALU.add).then_inc(y_biased, 1)
                    dve.wait_ge(y_biased, j + 1)
                    dve.tensor_scalar(Y[i], Y[i], slot_weight[:, bass.ds(j, 1)], None, ALU.mult).then_inc(y_weighted, 1)

                dve.wait_ge(w1_in, 16 * (E + 1))
                for j in range(2):
                    stage(j, j)
                weigh_slots()
                for j in range(2):
                    take_tokens(j, j)
                gather_weights()
                dve.wait_ge(b2_in, 16)
                over_blocks(dve, step)

            @block.tensor
            def _(pe):
                pe.wait_ge(ident_set, 1)
                for kind, args in EVENTS:
                    if kind == "pv":
                        if args == (0, 0, 0):
                            pe.wait_ge(ones_set, 1)
                        g, c, ps = args
                        b = g // GB
                        if ps == 0:
                            for q in (2 * c, 2 * c + 1):
                                for j in range(2):
                                    wait_consumed(pe, unit("exp_unit", g, q, j))
                            wait_consumed(pe, unit("v_proj", b, c // 2))
                        else:
                            pe.wait_ge(masked, UG * g + 2 * (c + 1))
                        if c == 0 and g >= 1:
                            pe.wait_ge(acc_saved[ps], g)
                        for i in range(GH):
                            n = 2 * UG * g + GH * c + i
                            last = pe.matmul(acc[ps][32 * i:32 * i + VW, :], V[b][:, c, GH * (g % GB) + i, :],
                                             (P1, P2)[ps][:, n % PRING, :], start=c == 0, stop=c == CT - 1)
                        last.then_inc(pv_done[ps], 1)
                        continue
                    if kind not in PSUM_KINDS:
                        continue
                    k = unit(kind, *args)
                    s = slot(k)
                    if k >= RING:
                        wait_consumed(pe, k - RING)
                    if kind in ("x_transpose", "t_transpose", "o_transpose", "gate_transpose"):
                        b, kc = args[0], args[-1]
                        src = O[args[1]] if kind == "o_transpose" else {"x_transpose": X, "t_transpose": T, "gate_transpose": X2}[kind]
                        if kind == "x_transpose":
                            pe.wait_ge(x_ready, b + 1)
                        elif kind == "gate_transpose":
                            pe.wait_ge(x2_ready, b + 1)
                        elif kind == "t_transpose":
                            pe.wait_ge(t_ready, b + 1)
                        else:
                            for g in range(GB * b, GB * b + GB):
                                wait_consumed(pe, unit("normalise", g, args[1]))
                        width, stride = (2 * GC, GC) if kind == "t_transpose" else (KW, KW)
                        for c in range(CT):
                            last = pe.transpose(s[0:width, c * P:(c + 1) * P], src[:, c, kc * stride:kc * stride + width],
                                                ident[:, :])
                    elif kind in ("q_proj", "k_proj"):
                        b, m = args
                        m0 = C * (kind == "k_proj") + m * GC
                        for kc in range(KC):
                            wait_consumed(pe, unit("x_transpose", b, kc))
                        if b == 0:
                            pe.wait_ge(wqkv_in, 32)
                            pe.wait_ge(consts_set, 1)
                        for kc in range(KC):
                            rows = KW + (kc == 0)
                            last = pe.matmul(s, WQKV[0:rows, kc, m0:m0 + 2 * GC], XT[0:rows, kc, :], start=kc == 0, stop=kc == KC - 1)
                    elif kind == "v_proj":
                        b, j = args
                        for kc in range(KC):
                            wait_consumed(pe, unit("x_transpose", b, kc))
                        for c in range(2):
                            for kc in range(KC):
                                rows = KW + (kc == 0)
                                last = pe.matmul(slot_tiles(k)[:, c, :], XT[0:rows, kc, (2 * j + c) * P:(2 * j + c + 1) * P],
                                                 WQKV[0:rows, kc, 2 * C:3 * C], start=kc == 0, stop=kc == KC - 1)
                    elif kind == "max_unit":
                        g, q, j = args
                        i, c, sl = (2 * q + j) % GH, q // 2, g % SLOTS[0]
                        if (q, j) == (0, 0):
                            for side in "qk":
                                pe.wait_ge(qk_loaded[side][sl], LOADS * (g // SLOTS[0] + 1))
                        last = pe.matmul(s, QS[0][sl][0:SD, i, c * P:(c + 1) * P], KS[0][sl][0:SD, i, :], start=True, stop=True)
                    elif kind == "exp_unit":
                        g, q, j = args
                        i, c, sl = (2 * q + j) % GH, q // 2, g % SLOTS[0]
                        if (g, q, j) == (0, 0, 0):
                            pe.wait_ge(stack_ones_set, SLOTS[0])
                        if (q, j) == (0, 0):
                            pe.wait_ge(row_loaded[sl], 32 * (g // SLOTS[0] + 1))
                        last = pe.matmul(s, KS[0][sl][:, i, c * P:(c + 1) * P], QS[0][sl][:, i, :], start=True, stop=True)
                    elif kind == "sim_unit":
                        g, q, j = args
                        i, c, sl = (2 * q + j) % GH, q // 2, g % SLOTS[1]
                        if (q, j) == (0, 0):
                            for side in "qk":
                                pe.wait_ge(sim_loaded[side][sl], LOADS * (g // SLOTS[1] + 1))
                        last = pe.matmul(s, QS[1][sl][:, i, c * P:(c + 1) * P], KS[1][sl][:, i, :], start=True, stop=True)
                    elif kind == "max_row":
                        g, = args
                        for q in range(UG - 2, UG):
                            for j in range(2):
                                wait_consumed(pe, unit("max_unit", g, q, j))
                        last = pe.transpose(s[0:4 * GH, 0:P], MX[:, g % 2, :], ident[:, :])
                    elif kind == "normalise":
                        g, ps = args
                        pe.wait_ge(acc_saved[ps], g + 1)
                        for c in range(CT):
                            last = pe.transpose(s[:, c * P:(c + 1) * P], ACCS[:, ps, c * P:(c + 1) * P], ident[:, :])
                    elif kind in ("proj_norm", "proj_out"):
                        b, j = args
                        norm = kind == "proj_norm"
                        for kc in range(KC):
                            wait_consumed(pe, unit("o_transpose", b, int(not norm), kc))
                        if b == 0:
                            pe.wait_ge(pw_in, 64)
                        for c in range(2):
                            for kc in range(KC):
                                rows = KW + (kc == 0)
                                last = pe.matmul(slot_tiles(k)[:, c, :], OT[0:rows, kc, (2 * j + c) * P:(2 * j + c + 1) * P],
                                                 (PWN if norm else PW)[0:rows, kc, :], start=kc == 0, stop=kc == KC - 1)
                    elif kind == "gate_logits":
                        b, = args
                        for kc in range(KC):
                            wait_consumed(pe, unit("gate_transpose", b, kc))
                        if b == 0:
                            pe.wait_ge(gt_in, 16)
                        for c in range(CT):
                            for kc in range(KC):
                                last = pe.matmul(s[:, c * E:(c + 1) * E], OT[0:KW, kc, c * P:(c + 1) * P], GT[:, kc, :],
                                                 start=kc == 0, stop=kc == KC - 1)
                    last.then_inc(filled[k % RING], 1)

                chose = rt["b"][:, :, :].rearrange("p t e -> p (t e)")
                pe.wait_ge(chosen, 1)
                pe.wait_ge(iotas_set, 1)
                pe.matmul(psum[:, 0, 0:P], before[:, :], chose, start=True, stop=True)
                pe.matmul(psum[:, 1, 0:P], ones[:, :], chose, start=True, stop=True).then_inc(counted, 1)
                pe.wait_ge(tags_ready, 1)
                for q in range(NQ):
                    pe.wait_ge(row_ready, q + 1)
                    last = pe.matmul(psum[:, 2, 0:2 * NBLK], oh_row[q // HQ][:, q % HQ, :], tag[:, q, :, :].rearrange("p s j -> p (s j)"),
                                     start=q == 0, stop=q == NQ - 1)
                last.then_inc(listed, 1)

                def turn(j, i):
                    pe.wait_ge(xg_loaded[i], 8 * (j + 2 - i))
                    wait_past(pe, xgt_ready, j - 1)
                    for kc in range(KC):
                        last = pe.transpose(xgt_ps[i][:, kc, :], XG[i][:, kc * KW:(kc + 1) * KW], ident[:, :])
                    last.then_inc(xgt_filled, 1)

                def first_layer(j, i):
                    pe.wait_ge(xgt_ready, j + 1)
                    pe.wait_ge(w1_staged, j + 1)
                    wait_past(pe, hid_done, j - 1)
                    for hc in range(HC):
                        for kc in range(KC):
                            rows = KW + (kc == 0)
                            last = pe.matmul(hid_ps[i][:, hc * P:(hc + 1) * P], W1S[i][0:rows, kc, hc * P:(hc + 1) * P],
                                             XGT[i][0:rows, kc, :], start=kc == 0, stop=kc == KC - 1)
                    last.then_inc(hid_filled, 1)

                def second_layer(j, i):
                    e = pe.value_load(blk_expert[0:1, bass.ds(j, 1)], min_val=0, max_val=E - 1)
                    pe.wait_ge(hid_done, j + 1)
                    wait_past(pe, y_weighted, j - 1)
                    if isinstance(j, int) and j == 1:
                        pe.wait_ge(weights_ready, 1)
                    for hc in range(HC):
                        last = pe.matmul(y_ps[i], HT[i][:, hc, :], w2_sb[:, bass.ds(e, 1), hc, :].rearrange("p o d -> p (o d)"),
                                         start=hc == 0, stop=hc == HC - 1)
                    last.then_inc(y_filled, 1)

                def step(j, i):
                    if not isinstance(j, int) or j + 2 < NBLK:
                        turn(j + 2, i)
                    if not isinstance(j, int) or j + 1 < NBLK:
                        first_layer(j + 1, (i + 1) % 2)
                    second_layer(j, i)

                pe.wait_ge(lists_ready, 1)
                turn(0, 0)
                turn(1, 1)
                for q in range(NQ):
                    if q % HQ == 0:
                        pe.wait_ge(wtags_ready, 3 * (q // HQ + 1))
                    last = pe.matmul(psum[:, 7, 0:3 * NBLK], oh_row[q // HQ][:, q % HQ, :],
                                     wtag[q // HQ][:, q % HQ, :, :].rearrange("p s j -> p (s j)"), start=q == 0, stop=q == NQ - 1)
                last.then_inc(weights_listed, 1)
                first_layer(0, 0)
                pe.wait_ge(w2_in, 16 * E)
                over_blocks(pe, step)


def kernel(x, L0_tok_tables, L0_tok_ln_scale, L0_tok_ln_bias, L0_attn_qkv_w, L0_attn_qkv_b, L0_attn_proj_w,
           L0_attn_proj_b, L0_ffn_gate_w, L0_ffn_w1, L0_ffn_b1, L0_ffn_w2, L0_ffn_b2):
    import numpy as np
    import concourse.bacc as bacc
    from concourse.bass_utils import run_bass_kernel_spmd

    primes = (31, 43, 59, 61, 73, 97, 103, 113)
    r = np.arange(BUCKETS)
    tables = np.asarray(L0_tok_tables)
    table = np.concatenate([tables[h][(r + 1) * p % BUCKETS] for h, p in enumerate(primes)], axis=1)
    by_width = np.arange(C).reshape(GB, GH, D).transpose(0, 2, 1).reshape(-1)
    qkv_cols = np.concatenate([by_width, C + by_width, 2 * C + np.arange(C)])
    proj_wt = np.asarray(L0_attn_proj_w).T
    arrays = {
        "ids": np.asarray(x), "table": table, "ln_scale": L0_tok_ln_scale, "ln_bias": L0_tok_ln_bias,
        "qkv_wt": np.asarray(L0_attn_qkv_w).T[:, qkv_cols], "qkv_b": np.asarray(L0_attn_qkv_b)[qkv_cols],
        "proj_wt": proj_wt, "proj_b": L0_attn_proj_b,
        "proj_wt_n": proj_wt[:, by_width], "proj_b_n": np.asarray(L0_attn_proj_b)[by_width],
        "gate_wt": np.asarray(L0_ffn_gate_w).T, "w1": L0_ffn_w1, "b1": L0_ffn_b1, "w2": L0_ffn_w2, "b2": L0_ffn_b2,
    }
    arrays = {k: np.ascontiguousarray(v) for k, v in arrays.items()}
    nc = bacc.Bacc("TRN2", target_bir_lowering=False, num_devices=1)
    args = [nc.dram_tensor(k, a.shape, mybir.dt.from_np(a.dtype), kind="ExternalInput").ap() for k, a in arrays.items()]
    result = nc.dram_tensor("result", (B * N + P, C), F32, kind="ExternalOutput").ap()
    build(nc, *args, result)
    r = run_bass_kernel_spmd(nc, [arrays], core_ids=[0])
    return r.results[0]["result"][:B * N].reshape(B, N, C)
```
